# Optimizing a Trainium2 kernel written in Bass

```python
import numpy as np
import jax
import jax.numpy as jnp

def _softmax(x, axis=-1):
    return jax.nn.softmax(x, axis=axis)

def _gelu(x):
    return jax.nn.gelu(x, approximate=True)

def _silu(x):
    return jax.nn.silu(x)

def _sigmoid(x):
    return jax.nn.sigmoid(x)

def _layernorm(x, axis=-1, eps=1e-05):
    m = jnp.mean(x, axis=axis, keepdims=True)
    v = jnp.var(x, axis=axis, keepdims=True)
    return (x - m) / jnp.sqrt(v + eps)

def _scatter_add(tgt, idx, src, axis=0):
    return tgt.at[idx].add(src)

def _segment_sum(src, seg, n):
    return jax.ops.segment_sum(src, seg, n)
kernel_name = 'mk_xattn_ffn_d1_seqx_r2_af06b2'

def setup_inputs(seed: int=0):
    np.random.seed(seed)
    _w = jnp.asarray

    def _rec_inputs():
        import jax
        import jax.numpy as jnp
        _rk = jax.random.key(seed)
        x = 7.22e-05 + 1 * jax.random.normal(jax.random.fold_in(_rk, 1), (16, 512, 512), jnp.float32)
        _lenS = 512 - jax.random.randint(jax.random.fold_in(_rk, 7), (16,), 0, max(1, 512 // 4) + 1, jnp.int32)
        _lenS2 = 512 - jax.random.randint(jax.random.fold_in(_rk, 8), (16,), 0, max(1, 512 // 4) + 1, jnp.int32)
        _ctx_1024P = jax.random.normal(jax.random.fold_in(_rk, 11), (16, 16, 512), jnp.float32)
        _ctx_1024c = jax.random.dirichlet(jax.random.fold_in(_rk, 511), 0.3 * jnp.ones((16,), jnp.float32), (16, 512))
        _ctx_1024t = jnp.einsum('bsk,bkd->bsd', _ctx_1024c, _ctx_1024P)
        _ctx_1024t = _ctx_1024t * jax.lax.rsqrt(jnp.mean(jnp.square(_ctx_1024t)) + 1e-12) * 0.953939
        ctx_1024 = 4.13588e-05 + 0.999923 * (_ctx_1024t + 0.3 * jax.random.normal(jax.random.fold_in(_rk, 611), (16, 512, 512), jnp.float32))
        _validS = jnp.arange(512)[None, :] < _lenS[:, None]
        _validS2 = jnp.arange(512)[None, :] < _lenS2[:, None]
        _causal = jnp.tril(jnp.ones((512, 512), dtype=bool))
        mask_Bx1x1xS2_if1 = jnp.where(jnp.ones((16, 1, 1, 512), dtype=bool), 1, 0).astype(jnp.int32)
        return (x, ctx_1024, mask_Bx1x1xS2_if1)
    x, ctx_1024, mask_Bx1x1xS2_if1 = _rec_inputs()

    def _L0_xattn_setup():
        import jax, jax.numpy as jnp
        import numpy as np
        import math
        D_MODEL = 512
        H = 16
        D_K = D_MODEL // H

        def _split_heads(x, B):
            return x.reshape(B, -1, H, D_K).transpose(0, 2, 1, 3)
        key = jax.random.key(seed)
        ks = jax.random.split(key, 12)
        B, S = (4, 1024)
        scale = 1.0 / math.sqrt(D_MODEL)
        inp = {'q': jax.random.normal(ks[0], (B, S, D_MODEL), jnp.float32), 'k': jax.random.normal(ks[1], (B, S, D_MODEL), jnp.float32), 'v': jax.random.normal(ks[2], (B, S, D_MODEL), jnp.float32), 'mask': jnp.ones((B, 1, 1, S), jnp.int32), 'wq': jax.random.normal(ks[3], (D_MODEL, D_MODEL), jnp.float32) * scale, 'bq': jax.random.normal(ks[4], (D_MODEL,), jnp.float32) * scale, 'wk': jax.random.normal(ks[5], (D_MODEL, D_MODEL), jnp.float32) * scale, 'bk': jax.random.normal(ks[6], (D_MODEL,), jnp.float32) * scale, 'wv': jax.random.normal(ks[7], (D_MODEL, D_MODEL), jnp.float32) * scale, 'bv': jax.random.normal(ks[8], (D_MODEL,), jnp.float32) * scale, 'wo': jax.random.normal(ks[9], (D_MODEL, D_MODEL), jnp.float32) * scale, 'bo': jax.random.normal(ks[10], (D_MODEL,), jnp.float32) * scale}
        return inp
    _L0_xattn_all = _L0_xattn_setup()
    _L0_xattn_in = {k: v for k, v in _L0_xattn_all.items() if k in ('wq', 'bq', 'wk', 'bk', 'wv', 'bv', 'wo', 'bo')}
    del _L0_xattn_all

    def _L0_ffn_setup():
        import jax, jax.numpy as jnp
        import numpy as np
        B, T, C, H, E = (4, 1024, 512, 1024, 8)
        CAPACITY_FACTOR = 1.0
        key = jax.random.key(seed)
        ks = jax.random.split(key, 5)
        scale = 0.02
        return {'x': jax.random.normal(ks[0], (B, T, C), dtype=jnp.float32), 'Wg': jax.random.normal(ks[1], (E, C), dtype=jnp.float32) * scale, 'W1': jax.random.normal(ks[2], (E, H, C), dtype=jnp.float32) * scale, 'W2': jax.random.normal(ks[3], (E, C, H), dtype=jnp.float32) * scale, 'W3': jax.random.normal(ks[4], (E, H, C), dtype=jnp.float32) * scale}
    _L0_ffn_all = _L0_ffn_setup()
    _L0_ffn_in = {k: v for k, v in _L0_ffn_all.items() if k in ('Wg', 'W1', 'W2', 'W3')}
    del _L0_ffn_all
    return {'x': x, 'ctx_1024': ctx_1024, 'mask_Bx1x1xS2_if1': mask_Bx1x1xS2_if1, 'L0_xattn_wq': _L0_xattn_in['wq'], 'L0_xattn_bq': _L0_xattn_in['bq'], 'L0_xattn_wk': _L0_xattn_in['wk'], 'L0_xattn_bk': _L0_xattn_in['bk'], 'L0_xattn_wv': _L0_xattn_in['wv'], 'L0_xattn_bv': _L0_xattn_in['bv'], 'L0_xattn_wo': _L0_xattn_in['wo'], 'L0_xattn_bo': _L0_xattn_in['bo'], 'L0_ffn_Wg': _L0_ffn_in['Wg'], 'L0_ffn_W1': _L0_ffn_in['W1'], 'L0_ffn_W2': _L0_ffn_in['W2'], 'L0_ffn_W3': _L0_ffn_in['W3']}

def reference(x, ctx_1024, mask_Bx1x1xS2_if1, L0_xattn_wq, L0_xattn_bq, L0_xattn_wk, L0_xattn_bk, L0_xattn_wv, L0_xattn_bv, L0_xattn_wo, L0_xattn_bo, L0_ffn_Wg, L0_ffn_W1, L0_ffn_W2, L0_ffn_W3):
    import jax
    import jax.numpy as jnp

    def _L0_xattn_ref(q, k, v, mask, wq, bq, wk, bk, wv, bv, wo, bo):
        import jax, jax.numpy as jnp
        import numpy as np
        import math
        D_MODEL = 512
        H = 16
        D_K = D_MODEL // H

        def _split_heads(x, B):
            return x.reshape(B, -1, H, D_K).transpose(0, 2, 1, 3)
        B = q.shape[0]
        qh = _split_heads(q @ wq.T + bq, B)
        kh = _split_heads(k @ wk.T + bk, B)
        vh = _split_heads(v @ wv.T + bv, B)
        scores = jnp.einsum('bhqd,bhkd->bhqk', qh, kh) / math.sqrt(D_K)
        scores = jnp.where(mask == 0, jnp.float32(-1000000000.0), scores)
        attn = jax.nn.softmax(scores, axis=-1)
        out = jnp.einsum('bhqk,bhkd->bhqd', attn, vh)
        out = out.transpose(0, 2, 1, 3).reshape(B, -1, D_MODEL)
        return out @ wo.T + bo

    def _L0_ffn_ref(x, Wg, W1, W2, W3):
        import jax, jax.numpy as jnp
        import numpy as np
        B, T, C, H, E = (4, 1024, 512, 1024, 8)
        CAPACITY_FACTOR = 1.0
        b, t, c = x.shape
        e = Wg.shape[0]
        n = b * t
        capacity = max(1, int(CAPACITY_FACTOR * n / e))
        x_flat = x.reshape(n, c)
        scores = (x_flat @ Wg.T).T
        top_vals, token_idx = jax.lax.top_k(scores, capacity)
        token_w = jax.nn.softmax(top_vals, axis=-1)
        xg = x_flat[token_idx]
        h = jax.nn.silu(jnp.einsum('eic,ehc->eih', xg, W1)) * jnp.einsum('eic,ehc->eih', xg, W3)
        y = jnp.einsum('eih,ech->eic', h, W2) * token_w[..., None]
        out = jnp.zeros_like(x_flat).at[token_idx.reshape(-1)].add(y.reshape(-1, c))
        return out.reshape(b, t, c)
    x = x + _L0_xattn_ref(_layernorm(x, axis=-1), ctx_1024, ctx_1024, mask_Bx1x1xS2_if1, L0_xattn_wq, L0_xattn_bq, L0_xattn_wk, L0_xattn_bk, L0_xattn_wv, L0_xattn_bv, L0_xattn_wo, L0_xattn_bo)
    x = x + _L0_ffn_ref(_layernorm(x, axis=-1), L0_ffn_Wg, L0_ffn_W1, L0_ffn_W2, L0_ffn_W3)
    return x

_drawn_inputs = setup_inputs


def setup_inputs(seed=0):
    import zlib

    import numpy as np

    out = dict(_drawn_inputs(seed))
    spreads = {}
    factors = {'L0_xattn_bq': 6.792,
     'L0_xattn_bk': 8.0,
     'L0_ffn_Wg': 8.0,
     'L0_ffn_W1': 8.0,
     'L0_ffn_W2': 8.0,
     'L0_ffn_W3': 8.0}
    for name, (base, spread) in spreads.items():
        noise = np.random.default_rng([zlib.crc32(name.encode()), seed]).standard_normal(out[name].shape)
        drawn = base * np.exp(spread * noise) if base else spread * noise
        out[name] = jnp.asarray(drawn.astype(out[name].dtype))
    for name, factor in factors.items():
        out[name] = (out[name] * factor).astype(out[name].dtype)
    return out
```

```python
from contextlib import ExitStack

import numpy as np

import concourse.bass as bass
from concourse import mybir

F32 = mybir.dt.float32
F32R = mybir.dt.float32r
BF16 = mybir.dt.bfloat16
I32 = mybir.dt.int32
U32 = mybir.dt.uint32
ALU = mybir.AluOpType
ACT = mybir.ActivationFunctionType
AX_X = mybir.AxisListType.X

P = 128
EPS = 1e-5
MASKED = -1e9
POOL_INIT = 6


def high_part(value):
    bits = np.float32(value).view(np.uint32) & np.uint32(0xFFFFF000)
    return float(bits.view(np.float32))


def over_batches(eng, batches, body):
    body(0, True, False)
    with eng.Fori(1, batches - 1) as b:
        body(b, False, False)
    body(batches - 1, False, True)


def attention(nc, x, ctxT, mask, wT, bq, bk, bv, bo, wgT, out, xn_dram, router_dram, q_parts, k_parts):
    B, S, D = x.shape
    H, DK = 16, 32
    CT = D // P
    KT = S // P
    HG = P // DK
    NG = H // HG
    QW = S // 2
    QT = QW // P
    UNITS = NG * 2
    E = wgT.shape[2]
    SCALE = float(DK) ** -0.5
    MASK_HI = high_part(MASKED / SCALE)
    MASK_LO = float(np.float32(MASKED / SCALE)) - MASK_HI
    ROWS_MASK = 3 * DK
    ROWS_MAX = ROWS_MASK + 2
    ROWS = ROWS_MAX + 2
    MX_ROWS = 16 * 2 * QT

    with ExitStack() as ctx:
        def sb(name, shape, dt=F32):
            return ctx.enter_context(nc.sbuf_tensor(name, shape, dt))

        def psum(name, shape):
            return ctx.enter_context(nc.psum_tensor(name, shape, F32))

        def sem(name):
            return ctx.enter_context(nc.semaphore(name))

        w_hi = {n: sb(f"w{n}_hi", [P, CT, D], F32R) for n in "qkvo"}
        w_lo = {n: sb(f"w{n}_lo", [P, CT, D], F32R) for n in "qkvo"}
        tok = sb("tok", [P, KT, D])
        xres = sb("xres", [P, 2, D])
        ctx_f = sb("ctx_f", [P, 2, S])
        ctx_hi = sb("ctx_hi", [P, CT, S], F32R)
        ctx_lo = sb("ctx_lo", [P, CT, S], F32R)
        xT_hi = sb("xT_hi", [P, CT, S], F32R)
        xT_lo = sb("xT_lo", [P, CT, S], F32R)
        v = sb("v", [P, KT, D])
        qs = sb("qs", [P, 2, HG, S], F32R)
        ks = sb("ks", [P, 2, HG, S], F32R)
        q_st = sb("q_st", [P, 2, S], F32R)
        k_f = sb("k_f", [P, S])
        k_st = sb("k_st", [P, 2, S], F32R)
        probs = sb("probs", [P, KT, HG, QW])
        psumk = sb("psumk", [P, HG, QW])
        recip = sb("recip", [P, QW])
        at_f = sb("at_f", [P, QW])
        at_hi = sb("at_hi", [P, NG, S], F32R)
        at_lo = sb("at_lo", [P, NG, S], F32R)
        keep = sb("keep", [P, S])
        bo_row = sb("bo_row", [P, D])
        ident = sb("ident", [P, P])
        mx = sb("mx", [P, P])
        mx_hi = sb("mx_hi", [HG * QT, P], F32R)
        mx_lo = sb("mx_lo", [HG * QT, P], F32R)
        rscore = sb("rscore", [E, P])
        wg = sb("wg", [P, CT, E])
        ones = sb("ones", [P, DK])
        b_q, b_k, b_v = (sb(f"b_{n}", [P, NG]) for n in "qkv")
        masked = sb("masked", [P, 1])
        stats = sb("stats", [P, KT, 6])
        mv = sb("mv", [P, KT, 2])
        rstd = sb("rstd", [P, 2, KT])
        half = sb("half", [P, KT])
        eps = sb("eps", [P, KT])
        xnT = k_f
        w_f = probs[:, :, :, :].rearrange("p k h q -> p (k h q)").rearrange("p (s c d) -> p s c d", s=2, d=D)

        ps_max = psum("ps_max", [P, 2, S])
        ps_exp = psum("ps_exp", [P, HG, QW])
        ps_av = [psum(f"ps_av{i}", [P, 2, QW]) for i in range(2)]
        ps_job = [psum(f"ps_job{i}", [P, 512]) for i in range(2)]

        consts_in = sem("consts_in")
        w_in = [sem(f"w_in{i}") for i in range(2)]
        w_hi_done = sem("w_hi_done")
        w_lo_done = sem("w_lo_done")
        pool_init = sem("pool_init")
        pool_zero = sem("pool_zero")
        stack_init = sem("stack_init")
        job_done = sem("job_done")
        sc_max = sem("sc_max")
        sc_exp = sem("sc_exp")
        av_done = sem("av_done")
        sum_done = sem("sum_done")
        mxT_done = sem("mxT_done")
        max_done = sem("max_done")
        mx_split = sem("mx_split")
        mx_rows = sem("mx_rows")
        exp_done = sem("exp_done")
        psumk_done = sem("psumk_done")
        recip_done = sem("recip_done")
        at_f_done = sem("at_f_done")
        at_hi_done = sem("at_hi_done")
        at_lo_done = sem("at_lo_done")
        q_hi_done, q_lo_done = sem("q_hi_done"), sem("q_lo_done")
        k_f_done, k_hi_done, k_lo_done = sem("k_f_done"), sem("k_hi_done"), sem("k_lo_done")
        q_spill, k_spill = sem("q_spill"), sem("k_spill")
        q_stack, k_stack = sem("q_stack"), sem("k_stack")
        keep_in = sem("keep_in")
        keep_done = sem("keep_done")
        row_done = sem("row_done")
        row_stack = sem("row_stack")
        v_done = sem("v_done")
        x_in = sem("x_in")
        bn1, mv1 = sem("bn1"), sem("mv1")
        rstd1 = sem("rstd1")
        xn1 = sem("xn1")
        xT_hi_done, xT_lo_done = sem("xT_hi_done"), sem("xT_lo_done")
        ctx_in = [sem(f"ctx_in{i}") for i in range(2)]
        ctx_hi_done, ctx_lo_done = sem("ctx_hi_done"), sem("ctx_lo_done")
        xres_in = [sem(f"xres_in{i}") for i in range(2)]
        xres_b = sem("xres_b")
        x2_done = sem("x2_done")
        x2_out = sem("x2_out")
        bn2, mv2 = sem("bn2"), sem("mv2")
        rstd2 = sem("rstd2")
        stats_seen = sem("stats_seen")
        xn2 = sem("xn2")
        xn2_out = sem("xn2_out")
        xnT_done = sem("xnT_done")
        rscore_done = sem("rscore_done")
        rscore_out = sem("rscore_out")

        JOBS = [
            [[("q", 2)], [("v", 3)], [("k", 2)], [], []],
            [[("o", 0)], [("o", 1)], [("o", 2)], [("o", 3)], []],
            [[], [], [("rt", 0)], [("rs", 0), ("rt", 1)], [("rs", 1), ("rt", 2)]],
            [[("rs", 2), ("rt", 3)], [("rs", 3), ("q", 3)], [("k", 3)], [], []],
            [[], [], [], [], [("lt", 0)]],
            [[("lt", 1), ("lt", 2)], [("lt", 3)], [("q", 0)], [("k", 0)], []],
            [[], [("q", 1)], [("k", 1)], [], []],
            [[], [], [("v", 0)], [("v", 1)], [("v", 2)]],
        ]
        OF_BATCH_BEFORE = ("o", "rt", "rs")
        OF_BATCH_AFTER = [("lt", t) for t in range(KT)] + [("q", 0), ("k", 0), ("q", 1), ("k", 1), ("v", 0), ("v", 1), ("v", 2)]
        PROLOGUE = OF_BATCH_AFTER
        EPILOGUE = [("o", t) for t in range(KT)] + [(k, t) for t in range(KT) for k in ("rt", "rs")]
        PER_BATCH = sum(len(place) for slot in JOBS for place in slot)
        JOBS_END = PER_BATCH * B - len(EPILOGUE)
        assert len(EPILOGUE) % 2 == 0 and PER_BATCH % 2 == 0

        def jobs_of(first, last):
            n, table = 0, []
            for u, places in enumerate(JOBS):
                table.append([])
                for place in places:
                    row = []
                    for kind, t in place:
                        if first and kind in OF_BATCH_BEFORE:
                            continue
                        if last and (kind, t) in OF_BATCH_AFTER:
                            continue
                        row.append((kind, t, n))
                        n += 1
                    table[-1].append(row)
            return table

        def job_base(b):
            return len(PROLOGUE) + PER_BATCH * b - (0 if isinstance(b, int) and b == 0 else len(EPILOGUE))

        def bank_of(n):
            return ps_job[(len(PROLOGUE) + n) % 2]

        def read_out(b, kind, t):
            return {
                "q": lambda: (q_lo_done, group(b, t) + 1),
                "k": lambda: (k_f_done, group(b, t) + 1),
                "v": lambda: (v_done, of_values(b, t)),
                "o": lambda: (x2_done, KT * (b - 1) + t + 1),
                "rt": lambda: (xnT_done, KT * (b - 1) + t + 1),
                "rs": lambda: (rscore_done, KT * (b - 1) + t + 1),
                "lt": lambda: (xT_lo_done, KT * (b + 1) + t + 1),
            }[kind]()

        def jobs_done(b, first, last, kind, t):
            for places in jobs_of(first, last):
                for row in places:
                    for k, a, n in row:
                        if (k, a) == (kind, t):
                            return job_base(b) + n + 1
            raise KeyError(kind)

        def need(eng, s, value):
            if not (isinstance(value, int) and value <= 0):
                eng.wait_ge(s, value)

        def group(b, t):
            return NG * (b + 1) + t if t < 2 else NG * b + t

        def of_values(b, t):
            return KT * (b + 1) + t + 1 if t < 3 else KT * b + t + 1

        block = ctx.enter_context(nc.Block())

        @block.sync
        def _(sp):
            def by_head(dram, part):
                return dram[:, part, :].rearrange("(h r) s -> r h s", r=DK)

            def rows(dram, b, t):
                return dram[bass.ds(b, 1), t * P:(t + 1) * P, :].rearrange("o p d -> p (o d)")

            def load_x(b):
                sp.dma_start(tok[:, :, :], x[bass.ds(b, 1)].rearrange("o (t p) d -> p (o t) d", p=P)).then_inc(x_in, 16)

            def load_keep(b):
                sp.dma_start(keep[:, :].bitcast(I32), mask[bass.ds(b, 1), :].broadcast_to([P, S])).then_inc(keep_in, 16)

            def load_ctx(b, t):
                sp.dma_start(ctx_f[:, t % 2, :], rows(ctxT, b, t)).then_inc(ctx_in[t % 2], 16)

            def load_residual(b, t):
                sp.dma_start(xres[:, t % 2, :], rows(x, b, t)).then_inc(xres_in[t % 2], 16)

            def spill_q(g, t):
                sp.wait_ge(q_hi_done, g + 1)
                sp.wait_ge(q_lo_done, g + 1)
                sp.dma_start(q_parts[t], q_st[:, :, :].bitcast(F32)).then_inc(q_spill, 16)

            def spill_k(g, t):
                sp.wait_ge(k_hi_done, g + 1)
                sp.wait_ge(k_lo_done, g + 1)
                sp.dma_start(k_parts[t], k_st[:, :, :].bitcast(F32)).then_inc(k_spill, 16)

            def stack(g, t):
                sp.wait_ge(q_spill, 16 * (g + 1))
                need(sp, sc_exp, KT * (2 * g - 2))
                for row, part in enumerate((0, 1, 0)):
                    sp.dma_start(qs[row * DK:(row + 1) * DK, t % 2, :, :].bitcast(F32), by_head(q_parts[t], part)).then_inc(q_stack, 16)
                sp.wait_ge(k_spill, 16 * (g + 1))
                for row, part in enumerate((0, 0, 1)):
                    sp.dma_start(ks[row * DK:(row + 1) * DK, t % 2, :, :].bitcast(F32), by_head(k_parts[t], part)).then_inc(k_stack, 16)

            def stack_row(b, par):
                sp.wait_ge(row_done, 2 * b + par + 1)
                for h in range(1, HG):
                    sp.dma_start(ks[ROWS_MASK:ROWS_MAX, par, h, :].bitcast(F32), ks[ROWS_MASK:ROWS_MAX, par, 0, :].bitcast(F32)).then_inc(row_stack, 16)

            def stack_max(unit, u):
                par, q0 = (u // 2) % 2, (u % 2) * QW
                sp.wait_ge(mx_split, 2 * unit + 2)
                for qt in range(QT):
                    q = slice(q0 + qt * P, q0 + (qt + 1) * P)
                    for row, src in ((0, mx_hi), (1, mx_lo)):
                        sp.dma_start(qs[ROWS_MAX + row:ROWS_MAX + row + 1, par, :, q].bitcast(F32),
                                     src[qt * HG:(qt + 1) * HG, :].bitcast(F32)).then_inc(mx_rows, 16)

            def store_x2(b, t):
                sp.wait_ge(x2_done, KT * b + t + 1)
                sp.dma_start(rows(out, b, t), tok[:, t, :]).then_inc(x2_out, 16)

            def store_xn(b):
                sp.wait_ge(xn2, KT * (b + 1))
                sp.dma_start(xn_dram[bass.ds(b, 1)].rearrange("o (t p) d -> p (o t) d", p=P), tok[:, :, :]).then_inc(xn2_out, 16)

            def store_router(b, t):
                sp.wait_ge(rscore_done, KT * b + t + 1)
                sp.dma_start(router_dram[bass.ds(b, 1), :, t * P:(t + 1) * P].rearrange("o e p -> e (o p)"), rscore[:, :]).then_inc(rscore_out, 16)

            load_x(0)
            load_ctx(0, 0)
            load_ctx(0, 1)
            for dst, src in ((b_q, bq), (b_k, bk), (b_v, bv)):
                sp.dma_start(dst[:, :], src).then_inc(consts_in, 16)
            sp.dma_start(bo_row[:, :], bo.rearrange("(o d) -> o d", o=1).broadcast_to([P, D])).then_inc(consts_in, 16)
            sp.dma_start(wg[:, :, :], wgT).then_inc(consts_in, 16)
            load_keep(0)
            for n, name in enumerate("qkvo"):
                if n >= 2:
                    sp.wait_ge(w_lo_done, n - 1)
                sp.dma_start(w_f[:, n % 2], wT[name].rearrange("(c p) d -> p c d", p=P)).then_inc(w_in[n % 2], 16)
                if n < 2:
                    sp.wait_ge(ctx_lo_done, n + 1)
                    load_ctx(0, n + 2)
            stack_row(0, 0)
            spill_q(0, 0)
            spill_k(0, 0)
            stack(0, 0)
            spill_q(1, 1)
            spill_k(1, 1)
            stack_max(0, 0)

            def body(b, first, last):
                table = jobs_of(first, last)
                for u in range(UNITS):
                    unit, next_u = UNITS * b + u, (u + 1) % UNITS
                    made = [(kind, t) for place in table[u] for kind, t, _ in place]
                    if u % 2 == 0 and not (last and u == 6):
                        t = (u // 2 + 1) % NG
                        stack(NG * b + u // 2 + 1, t)
                    if u == 0:
                        stack_row(b, 1)
                    if u == 6 and not last:
                        stack_row(b + 1, 0)
                    if u == 0 and not first:
                        load_residual(b - 1, 0)
                        load_residual(b - 1, 1)
                    if u == 1 and not first:
                        for t in range(2):
                            store_x2(b - 1, t)
                            load_residual(b - 1, t + 2)
                    if u == 3 and not first:
                        sp.wait_ge(xn2_out, 16 * b)
                        for t in range(1, KT):
                            store_router(b - 1, t)
                        sp.wait_ge(rscore_out, 16 * KT * b)
                    if u == 3 and first:
                        sp.wait_ge(job_done, KT)
                    if u == 3 and not last:
                        load_x(b + 1)
                    if u == 4 and not last:
                        sp.wait_ge(k_f_done, NG * b + NG)
                        load_keep(b + 1)
                        for t in range(CT):
                            sp.wait_ge(ctx_lo_done, CT * (b + 1) + t - 1)
                            load_ctx(b + 1, t)
                    for kind, t in made:
                        if kind == "q":
                            spill_q(group(b, t), t)
                    if not (last and u == UNITS - 1):
                        stack_max(unit + 1, next_u)
                    for kind, t in made:
                        if kind == "k":
                            spill_k(group(b, t), t)
                    if u == 1 and not first:
                        store_x2(b - 1, 2)
                        store_x2(b - 1, 3)
                    if u == 2 and not first:
                        store_xn(b - 1)
                        store_router(b - 1, 0)

            over_batches(sp, B, body)
            load_residual(B - 1, 0)
            load_residual(B - 1, 1)
            for t in range(KT):
                store_x2(B - 1, t)
                if t + 2 < KT:
                    load_residual(B - 1, t + 2)
            store_xn(B - 1)
            for t in range(KT):
                store_router(B - 1, t)
            sp.wait_ge(x2_out, 16 * KT * B)
            sp.wait_ge(xn2_out, 16 * B)
            sp.wait_ge(rscore_out, 16 * KT * B)

        @block.tensor
        def _(pe):
            def product3(dst, a_hi, a_lo, b_hi, b_lo):
                for c in range(CT):
                    for i, (l, r) in enumerate(((a_hi, b_hi), (a_hi, b_lo), (a_lo, b_hi))):
                        last = nc.tensor.matmul(dst, l(c), r(c), start=(c == 0 and i == 0), stop=(c == CT - 1 and i == 2))
                return last

            def job(b, kind, t, bank, before):
                if before is not None:
                    pe.wait_ge(*before)
                if kind in "qk":
                    g = slice(t * P, (t + 1) * P)
                    if kind == "q":
                        src_hi, src_lo = xT_hi, xT_lo
                    else:
                        src_hi, src_lo = ctx_hi, ctx_lo
                    if t < 2:
                        nb = b + 1
                        if kind == "q":
                            pe.wait_ge(xT_lo_done, KT * (nb + 1))
                        else:
                            pe.wait_ge(ctx_lo_done, CT * (nb + 1))
                    wh, wl = w_hi[kind], w_lo[kind]
                    last = product3(bank[:, :], lambda c: wh[:, c, g], lambda c: wl[:, c, g],
                                    lambda c: src_hi[:, c, :], lambda c: src_lo[:, c, :])
                elif kind == "v":
                    s = slice(t * P, (t + 1) * P)
                    last = product3(bank[:, :], lambda c: ctx_hi[:, c, s], lambda c: ctx_lo[:, c, s],
                                    lambda c: w_hi["v"][:, c, :], lambda c: w_lo["v"][:, c, :])
                elif kind == "o":
                    s = slice(t * P, (t + 1) * P)
                    if t == 0:
                        pe.wait_ge(at_lo_done, UNITS * b)
                    last = product3(bank[:, :], lambda c: at_hi[:, c, s], lambda c: at_lo[:, c, s],
                                    lambda c: w_hi["o"][:, c, :], lambda c: w_lo["o"][:, c, :])
                elif kind in ("lt", "rt"):
                    if kind == "lt":
                        pe.wait_ge(xn1, KT * (b + 1) + t + 1)
                    else:
                        pe.wait_ge(xn2, KT * (b - 1) + t + 1)
                    for c in range(CT):
                        last = nc.tensor.matmul(bank[:, c * P:(c + 1) * P], tok[:, t, c * P:(c + 1) * P], ident[:, :],
                                                is_transpose=True, start=True, stop=True)
                elif kind == "rs":
                    pe.wait_ge(xnT_done, KT * (b - 1) + t + 1)
                    for c in range(CT):
                        last = nc.tensor.matmul(bank[0:E, 0:P], wg[:, c, :], xnT[:, c * P:(c + 1) * P],
                                                start=(c == 0), stop=(c == CT - 1))
                last.then_inc(job_done, 1)

            def scores_max(unit, u, pair):
                par, q0 = (u // 2) % 2, (u % 2) * QW
                if pair == 0:
                    need(pe, mx_split, 2 * unit)
                else:
                    pe.wait_ge(max_done, HG * unit + pair)
                for qt in range(QT):
                    q = slice(q0 + qt * P, q0 + (qt + 1) * P)
                    last = nc.tensor.matmul(ps_max[:, qt, :], qs[0:ROWS_MAX, par, pair, q], ks[0:ROWS_MAX, par, pair, :],
                                            start=True, stop=True)
                last.then_inc(sc_max, 1)

            def scores_exp(unit, u, kt):
                par, q0 = (u // 2) % 2, (u % 2) * QW
                if kt == 0:
                    pe.wait_ge(mx_rows, MX_ROWS * (unit + 1))
                need(pe, exp_done, KT * unit + kt)
                for h in range(HG):
                    last = nc.tensor.matmul(ps_exp[:, h, :], ks[0:ROWS, par, h, kt * P:(kt + 1) * P],
                                            qs[0:ROWS, par, h, q0:q0 + QW], start=True, stop=True)
                last.then_inc(sc_exp, 1)

            def maxima(unit):
                pe.wait_ge(max_done, HG * unit + HG)
                nc.tensor.matmul(ps_max[:, 0, 0:P], mx[:, :], ident[:, :], is_transpose=True, start=True, stop=True).then_inc(mxT_done, 1)

            def probs_v(unit, u, b, kt, av_bank):
                g = u // 2
                pe.wait_ge(exp_done, KT * unit + kt + 1)
                if kt == 0:
                    need(pe, at_f_done, unit - 1)
                if u == 0:
                    pe.wait_ge(v_done, KT * b + kt + 1)
                for h in range(HG):
                    last = nc.tensor.matmul(ps_av[av_bank][h * DK:(h + 1) * DK, 0, :],
                                            v[:, kt, (g * HG + h) * DK:(g * HG + h + 1) * DK], probs[:, kt, h, :],
                                            start=(kt == 0), stop=(kt == KT - 1), tile_position=(0, h * DK))
                last.then_inc(av_done, 1)

            def sums(unit, av_bank):
                pe.wait_ge(psumk_done, 3 * unit + 3)
                for h in range(HG):
                    last = nc.tensor.matmul(ps_av[av_bank][h * DK:(h + 1) * DK, 1, :], ones[:, :], psumk[:, h, :],
                                            start=True, stop=True, tile_position=(0, h * DK))
                last.then_inc(sum_done, 1)

            pe.wait_ge(consts_in, 5 * 16)
            pe.wait_ge(pool_init, POOL_INIT)
            pe.wait_ge(w_lo_done, 4)
            for n, (kind, t) in enumerate(PROLOGUE):
                job(-1, kind, t, ps_job[n % 2], read_out(-1, *PROLOGUE[n - 2]) if n >= 2 else None)
            pe.wait_ge(q_stack, 3 * 16)
            pe.wait_ge(k_stack, 3 * 16)
            pe.wait_ge(row_stack, 3 * 16)
            for pair in range(HG):
                scores_max(0, 0, pair)
            maxima(0)

            def body(b, first, last):
                table = jobs_of(first, last)
                order = [(kind, t) for places in table for row in places for kind, t, _ in row]
                for u in range(UNITS):
                    unit = UNITS * b + u
                    has_next = not (last and u == UNITS - 1)
                    nu = (u + 1) % UNITS
                    has_prev = not (first and u == 0)
                    bank, prev_bank = u % 2, (u + 1) % 2

                    def fill(place):
                        for kind, t, n in table[u][place]:
                            before = read_out(b, *order[n - 2]) if n >= 2 else read_out(b - 1, *PROLOGUE[n - 2])
                            job(b, kind, t, bank_of(n), before)

                    if has_next:
                        if u % 2 == 1:
                            g = NG * b + u // 2 + 1
                            pe.wait_ge(q_stack, 48 * g + 48)
                            pe.wait_ge(k_stack, 48 * g + 48)
                            if u == 1:
                                pe.wait_ge(row_stack, 96 * b + 96)
                            if u == UNITS - 1:
                                pe.wait_ge(row_stack, 96 * b + 96 + 48)
                        scores_max(unit + 1, nu, 0)
                    if has_prev:
                        probs_v(unit - 1, (u - 1) % UNITS, b - 1 if u == 0 else b, KT - 1, prev_bank)
                    fill(0)
                    scores_exp(unit, u, 0)
                    if has_next:
                        scores_max(unit + 1, nu, 1)
                    fill(1)
                    scores_exp(unit, u, 1)
                    if has_next:
                        scores_max(unit + 1, nu, 2)
                    if has_prev:
                        sums(unit - 1, prev_bank)
                    probs_v(unit, u, b, 0, bank)
                    scores_exp(unit, u, 2)
                    if has_next:
                        scores_max(unit + 1, nu, 3)
                    fill(2)
                    probs_v(unit, u, b, 1, bank)
                    if has_next:
                        maxima(unit + 1)
                    scores_exp(unit, u, 3)
                    fill(3)
                    probs_v(unit, u, b, 2, bank)
                    fill(4)

            over_batches(pe, B, body)
            end = UNITS * B - 1
            probs_v(end, UNITS - 1, B - 1, KT - 1, end % 2)
            sums(end, end % 2)
            last_jobs = [(kind, t) for places in jobs_of(False, True) for row in places for kind, t, _ in row]
            for n, (kind, t) in enumerate(EPILOGUE):
                before = read_out(B, *EPILOGUE[n - 2]) if n >= 2 else read_out(B - 1, *last_jobs[n - 2])
                job(B, kind, t, ps_job[(JOBS_END + n) % 2], before)

        @block.scalar
        def _(act):
            def read(b, kind, t, bank, done):
                g = group(b, t) if kind in ("q", "k") else None
                if kind == "q":
                    act.wait_ge(job_done, done)
                    need(act, q_spill, 16 * g)
                    nc.scalar.activation(q_st[:, 0, :], bank[:, :], ACT.Identity, bias=b_q[:, t:t + 1]).then_inc(q_hi_done, 1)
                elif kind == "k":
                    act.wait_ge(k_f_done, g + 1)
                    need(act, k_spill, 16 * g)
                    nc.scalar.activation(k_st[:, 0, :], k_f[:, :], ACT.Copy).then_inc(k_hi_done, 1)
                elif kind == "v":
                    act.wait_ge(job_done, done)
                    need(act, av_done, KT * (UNITS * (b + (1 if t < 3 else 0)) - 1) + t + 1)
                    nc.scalar.activation(v[:, t, :], bank[:, :], ACT.Copy).then_inc(v_done, 1)
                elif kind == "lt":
                    act.wait_ge(job_done, done)
                    nc.scalar.activation(xT_hi[:, :, t * P:(t + 1) * P], bank[:, :].rearrange("p (c q) -> p c q", c=CT), ACT.Copy).then_inc(xT_hi_done, 1)
                elif kind == "rt":
                    act.wait_ge(job_done, done)
                    if t == 0:
                        act.wait_ge(k_lo_done, NG * b + (0 if isinstance(b, int) and b == B else 3))
                    nc.scalar.activation(xnT[:, :], bank[:, :], ACT.Copy).then_inc(xnT_done, 1)

            def split_ctx(b, t, uses):
                act.wait_ge(ctx_in[t % 2], 16 * (2 * b + t // 2 + 1))
                if uses is not None:
                    act.wait_ge(job_done, uses)
                nc.scalar.activation(ctx_hi[:, t, :], ctx_f[:, t % 2, :], ACT.Copy).then_inc(ctx_hi_done, 1)

            def split_w(n, name):
                act.wait_ge(w_in[n % 2], 16 * (n // 2 + 1))
                nc.scalar.activation(w_hi[name][:, :, :], w_f[:, n % 2], ACT.Copy).then_inc(w_hi_done, 1)

            def exponentials(unit, kt):
                act.wait_ge(sc_exp, KT * unit + kt + 1)
                need(act, av_done, KT * (unit - 1) + kt + 1)
                need(act, psumk_done, 3 * (unit - 1) + max(1, kt))
                nc.scalar.activation(probs[:, kt, :, :], ps_exp[:, :, :], ACT.Exp, scale=SCALE).then_inc(exp_done, 1)

            def output_hi(unit, u, o_done):
                g, q = u // 2, slice((u % 2) * QW, (u % 2 + 1) * QW)
                act.wait_ge(at_f_done, unit + 1)
                if o_done is not None:
                    act.wait_ge(job_done, o_done)
                nc.scalar.activation(at_hi[:, g, q], at_f[:, :], ACT.Identity, bias=b_v[:, g:g + 1]).then_inc(at_hi_done, 1)

            act.wait_ge(consts_in, 5 * 16)
            split_ctx(0, 0, None)
            split_ctx(0, 1, None)
            split_w(0, "q")
            split_ctx(0, 2, None)
            split_w(1, "k")
            split_ctx(0, 3, None)
            split_w(2, "v")
            split_w(3, "o")
            for n, (kind, t) in enumerate(PROLOGUE):
                read(-1, kind, t, ps_job[n % 2], n + 1)

            def body(b, first, last):
                table = jobs_of(first, last)
                for u in range(UNITS):
                    unit = UNITS * b + u

                    def fill(place):
                        for kind, t, n in table[u][place]:
                            read(b, kind, t, bank_of(n), job_base(b) + n + 1)

                    def next_ctx(t):
                        if u == 4 and not last:
                            split_ctx(b + 1, t, jobs_done(b, first, last, "k", 3))

                    fill(0)
                    exponentials(unit, 0)
                    next_ctx(0)
                    fill(1)
                    exponentials(unit, 1)
                    next_ctx(1)
                    exponentials(unit, 2)
                    next_ctx(2)
                    fill(2)
                    exponentials(unit, 3)
                    fill(3)
                    if not (first and u == 0):
                        writes = None
                        if not first and u in (1, 2):
                            writes = jobs_done(b, first, last, "o", 1 if u == 1 else 3)
                        output_hi(unit - 1, (u - 1) % UNITS, writes)
                    next_ctx(3)
                    fill(4)

            over_batches(act, B, body)
            output_hi(UNITS * B - 1, UNITS - 1, None)
            for n, (kind, t) in enumerate(EPILOGUE):
                read(B, kind, t, ps_job[(JOBS_END + n) % 2], JOBS_END + n + 1)

        @block.vector
        def _(dve):
            def read(b, kind, t, bank, done):
                if kind == "q":
                    g = group(b, t)
                    dve.wait_ge(q_hi_done, g + 1)
                    need(dve, q_spill, 16 * g)
                    nc.vector.scalar_tensor_tensor(out=q_st[:, 1, :], in0=bank[:, :], scalar=b_q[:, t:t + 1], in1=q_st[:, 0, :].bitcast(F32),
                                                   op0=ALU.add, op1=ALU.subtract).then_inc(q_lo_done, 1)
                elif kind == "k":
                    g = group(b, t)
                    dve.wait_ge(job_done, done)
                    need(dve, k_hi_done, g)
                    need(dve, k_lo_done, g)
                    nc.vector.scalar_tensor_tensor(out=k_f[:, :], in0=bank[:, :], scalar=b_k[:, t:t + 1], in1=keep[:, :],
                                                   op0=ALU.add, op1=ALU.mult).then_inc(k_f_done, 1)
                elif kind == "o":
                    dve.wait_ge(job_done, done)
                    dve.wait_ge(xres_b, KT * (b - 1) + t + 1)
                    nc.vector.tensor_tensor(out=tok[:, t, :], in0=bank[:, :], in1=xres[:, t % 2, :], op=ALU.add).then_inc(x2_done, 1)
                    dve.wait_ge(x2_done, KT * (b - 1) + t + 1)
                    nc.vector.bn_stats(out=stats[:, t, :], in_=tok[:, t, :]).then_inc(bn2, 1)
                    if t == KT - 1:
                        dve.wait_ge(bn2, KT * b)
                        dve.sem_inc(stats_seen, 1)
                        for i in range(KT):
                            nc.vector.bn_aggr(out=mv[:, i, :], in_=stats[:, i, :]).then_inc(mv2, 1)
                elif kind == "rs":
                    dve.wait_ge(job_done, done)
                    if t > 0:
                        dve.wait_ge(rscore_out, 16 * (KT * (b - 1) + t))
                    nc.vector.tensor_copy(rscore[:, :], bank[0:E, 0:P]).then_inc(rscore_done, 1)
                elif kind == "lt":
                    dve.wait_ge(xT_hi_done, KT * (b + 1) + t + 1)
                    s = slice(t * P, (t + 1) * P)
                    nc.vector.tensor_tensor(out=xT_lo[:, :, s], in0=bank[:, :].rearrange("p (c q) -> p c q", c=CT),
                                            in1=xT_hi[:, :, s].bitcast(F32), op=ALU.subtract).then_inc(xT_lo_done, 1)

            def keep_from_mask(b):
                dve.wait_ge(keep_in, 16 * (b + 1))
                nc.vector.tensor_scalar(out=keep[:, :], in0=keep[:, :].bitcast(I32), scalar1=0, scalar2=None,
                                        op0=ALU.not_equal).then_inc(keep_done, 1)

            def mask_row(b, par):
                dve.wait_ge(keep_done, b + 1)
                need(dve, sc_exp, KT * (UNITS * (b - 1) + 6 + 2 * par))
                nc.vector.tensor_scalar(out=ks[ROWS_MASK:ROWS_MAX, par, 0, :], in0=keep[ROWS_MASK:ROWS_MAX, :], scalar1=0.0,
                                        scalar2=masked[ROWS_MASK:ROWS_MAX, :], op0=ALU.is_equal, op1=ALU.mult).then_inc(row_done, 1)

            def maximum(unit, pair):
                dve.wait_ge(sc_max, HG * unit + pair + 1)
                nc.vector.tensor_reduce(out=mx[:, pair:HG * QT:HG], in_=ps_max[:, :, :], axis=AX_X, op=ALU.max).then_inc(max_done, 1)

            def split_maxima(unit):
                dve.wait_ge(mxT_done, unit + 1)
                need(dve, mx_rows, MX_ROWS * unit)
                nc.vector.tensor_copy(mx_hi[:, :], ps_max[0:HG * QT, 0, 0:P]).then_inc(mx_split, 1)
                dve.wait_ge(mx_split, 2 * unit + 1)
                nc.vector.tensor_tensor(out=mx_lo[:, :], in0=ps_max[0:HG * QT, 0, 0:P], in1=mx_hi[:, :].bitcast(F32),
                                        op=ALU.subtract).then_inc(mx_split, 1)

            def normalise(unit, av_bank):
                dve.wait_ge(sum_done, unit + 1)
                nc.vector.reciprocal(recip[:, :], ps_av[av_bank][:, 1, :]).then_inc(recip_done, 1)
                dve.wait_ge(recip_done, unit + 1)
                nc.vector.tensor_tensor(out=at_f[:, :], in0=ps_av[av_bank][:, 0, :], in1=recip[:, :], op=ALU.mult).then_inc(at_f_done, 1)

            def output_lo(unit, u):
                g, q = u // 2, slice((u % 2) * QW, (u % 2 + 1) * QW)
                dve.wait_ge(at_hi_done, unit + 1)
                nc.vector.scalar_tensor_tensor(out=at_lo[:, g, q], in0=at_f[:, :], scalar=b_v[:, g:g + 1], in1=at_hi[:, g, q].bitcast(F32),
                                               op0=ALU.add, op1=ALU.subtract).then_inc(at_lo_done, 1)

            def statistics(b):
                dve.wait_ge(x_in, 16 * (b + 1))
                for t in range(KT):
                    nc.vector.bn_stats(out=stats[:, t, :], in_=tok[:, t, :]).then_inc(bn1, 1)
                dve.wait_ge(bn1, KT * (b + 1))
                dve.sem_inc(stats_seen, 1)
                for t in range(KT):
                    nc.vector.bn_aggr(out=mv[:, t, :], in_=stats[:, t, :]).then_inc(mv1, 1)

            def apply_norm(which, done):
                for t in range(KT):
                    nc.vector.tensor_scalar(out=tok[:, t, :], in0=tok[:, t, :], scalar1=mv[:, t, 0:1], scalar2=rstd[:, which, t:t + 1],
                                            op0=ALU.subtract, op1=ALU.mult).then_inc(done, 1)

            dve.wait_ge(consts_in, 5 * 16)
            dve.wait_ge(pool_init, POOL_INIT)
            nc.vector.memset(qs[ROWS_MASK:P, :, :, :].bitcast(F32), 1.0).then_inc(stack_init, 1)
            nc.vector.memset(ks[ROWS_MASK:P, :, :, :].bitcast(F32), -1.0).then_inc(stack_init, 1)
            statistics(0)
            dve.wait_ge(stack_init, 2)
            keep_from_mask(0)
            mask_row(0, 0)
            for n, name in enumerate("qkvo"):
                dve.wait_ge(w_hi_done, n + 1)
                nc.vector.tensor_tensor(out=w_lo[name][:, :, :], in0=w_f[:, n % 2], in1=w_hi[name][:, :, :].bitcast(F32),
                                        op=ALU.subtract).then_inc(w_lo_done, 1)
                if n == 1:
                    dve.wait_ge(rstd1, 2)
                    apply_norm(0, xn1)
            for n, (kind, t) in enumerate(PROLOGUE):
                read(-1, kind, t, ps_job[n % 2], n + 1)
            for pair in range(HG):
                maximum(0, pair)
            split_maxima(0)

            def body(b, first, last):
                table = jobs_of(first, last)
                for u in range(UNITS):
                    unit = UNITS * b + u
                    has_next = not (last and u == UNITS - 1)
                    has_prev = not (first and u == 0)

                    def fill(place):
                        for kind, t, n in table[u][place]:
                            read(b, kind, t, bank_of(n), job_base(b) + n + 1)

                    if u == 0:
                        mask_row(b, 1)
                    if u == 5 and not last:
                        keep_from_mask(b + 1)
                    if u == 6 and not last:
                        mask_row(b + 1, 0)
                    if has_next:
                        maximum(unit + 1, 0)
                    if u == 4 and not last:
                        statistics(b + 1)
                    fill(0)
                    if has_next:
                        maximum(unit + 1, 1)
                    fill(1)
                    if has_next:
                        maximum(unit + 1, 2)
                    if u == 2 and not first:
                        dve.wait_ge(x2_out, 16 * KT * b)
                        dve.wait_ge(rstd2, 2 * b)
                        apply_norm(1, xn2)
                    if has_next:
                        maximum(unit + 1, 3)
                    fill(2)
                    if has_next:
                        split_maxima(unit + 1)
                    if has_prev:
                        normalise(unit - 1, (u + 1) % 2)
                    fill(3)
                    if has_prev:
                        output_lo(unit - 1, (u - 1) % UNITS)
                    if u == 4 and not last:
                        dve.wait_ge(rstd1, 2 * (b + 2))
                        apply_norm(0, xn1)
                    fill(4)

            over_batches(dve, B, body)
            end = UNITS * B - 1
            normalise(end, end % 2)
            output_lo(end, UNITS - 1)
            for n, (kind, t) in enumerate(EPILOGUE):
                read(B, kind, t, ps_job[(JOBS_END + n) % 2], JOBS_END + n + 1)
                if (kind, t) == ("o", KT - 1):
                    dve.wait_ge(x2_out, 16 * KT * B)
                    dve.wait_ge(rstd2, 2 * B)
                    apply_norm(1, xn2)

        @block.gpsimd
        def _(pool):
            def inverse_sigma(which, stats_done, count, done, made):
                pool.wait_ge(stats_done, count)
                nc.gpsimd.tensor_tensor(out=rstd[:, which, :], in0=mv[:, :, 1], in1=eps[:, :], op=ALU.add).then_inc(done, 1)
                pool.wait_ge(done, made + 1)
                nc.gpsimd.tensor_tensor(out=rstd[:, which, :], in0=rstd[:, which, :], in1=half[:, :], op=ALU.pow).then_inc(done, 1)

            def ctx_rest(b, t):
                pool.wait_ge(ctx_hi_done, CT * b + t + 1)
                nc.gpsimd.tensor_tensor(out=ctx_lo[:, t, :], in0=ctx_f[:, t % 2, :], in1=ctx_hi[:, t, :].bitcast(F32),
                                        op=ALU.subtract).then_inc(ctx_lo_done, 1)

            def k_rest(g):
                pool.wait_ge(k_hi_done, g + 1)
                need(pool, k_spill, 16 * g)
                nc.gpsimd.tensor_tensor(out=k_st[:, 1, :], in0=k_f[:, :], in1=k_st[:, 0, :].bitcast(F32), op=ALU.subtract).then_inc(k_lo_done, 1)

            def residual_bias(b, t):
                pool.wait_ge(xres_in[t % 2], 16 * (2 * b + t // 2 + 1))
                nc.gpsimd.tensor_tensor(out=xres[:, t % 2, :], in0=xres[:, t % 2, :], in1=bo_row[:, :], op=ALU.add).then_inc(xres_b, 1)

            def add_up(unit, step):
                pool.wait_ge(exp_done, KT * unit + step + 2)
                if step == 0:
                    need(pool, sum_done, unit)
                else:
                    pool.wait_ge(psumk_done, 3 * unit + step)
                nc.gpsimd.tensor_tensor(out=psumk[:, :, :], in0=probs[:, 0] if step == 0 else psumk[:, :, :], in1=probs[:, step + 1],
                                        op=ALU.add).then_inc(psumk_done, 1)

            nc.gpsimd.memset(ident[:, :], 0.0).then_inc(pool_zero, 1)
            nc.gpsimd.memset(masked[:, :], MASK_HI).then_inc(pool_zero, 1)
            nc.gpsimd.memset(half[:, :], -0.5).then_inc(pool_init, 1)
            nc.gpsimd.memset(eps[:, :], EPS).then_inc(pool_init, 1)
            nc.gpsimd.memset(ones[:, :], 1.0).then_inc(pool_init, 1)
            nc.gpsimd.memset(mx[:, :], 0.0).then_inc(pool_init, 1)
            pool.wait_ge(pool_zero, 2)
            nc.gpsimd.affine_select(out=ident[:, :], in_=ident[:, :], compare_op=ALU.not_equal, fill=1.0, base=0,
                                    pattern=[[-1, P]], channel_multiplier=1).then_inc(pool_init, 1)
            nc.gpsimd.affine_select(out=masked[:, :], in_=masked[:, :], compare_op=ALU.not_equal, fill=MASK_LO, base=-(ROWS_MASK + 1),
                                    pattern=[[0, 1]], channel_multiplier=1).then_inc(pool_init, 1)
            inverse_sigma(0, mv1, KT, rstd1, 0)
            for t in range(CT):
                ctx_rest(0, t)
            pool.wait_ge(consts_in, 5 * 16)
            k_rest(0)
            k_rest(1)

            def body(b, first, last):
                table = jobs_of(first, last)
                for u in range(UNITS):
                    unit = UNITS * b + u

                    def keys(*places):
                        for place in places:
                            for kind, t, _ in table[u][place]:
                                if kind == "k":
                                    k_rest(group(b, t))

                    def next_ctx(t):
                        if u == 4 and not last:
                            ctx_rest(b + 1, t)

                    def residual(t):
                        if u == 1 and not first:
                            residual_bias(b - 1, t)

                    residual(0)
                    residual(1)
                    if u == 2 and not first:
                        inverse_sigma(1, mv2, KT * b, rstd2, 2 * (b - 1))
                    next_ctx(0)
                    if u == 4 and not last:
                        inverse_sigma(0, mv1, KT * (b + 2), rstd1, 2 * (b + 1))
                    add_up(unit, 0)
                    keys(0, 1)
                    residual(2)
                    next_ctx(1)
                    add_up(unit, 1)
                    keys(2)
                    residual(3)
                    next_ctx(2)
                    add_up(unit, 2)
                    next_ctx(3)
                    keys(3, 4)

            over_batches(pool, B, body)
            for t in range(KT):
                residual_bias(B - 1, t)
            inverse_sigma(1, mv2, KT * B, rstd2, 2 * (B - 1))


def route_constants(batches, experts, tiles):
    row = np.arange(P)
    same = (row[:, None] % experts == row[None, :] % experts).astype(np.float32)
    before = same * (row[:, None] < row[None, :])
    numbers = np.broadcast_to(row[None, :], (P, P))
    tile_ids = np.broadcast_to(np.arange(batches * tiles)[None, :], (P, batches * tiles))
    return np.concatenate([same, before, np.eye(P), numbers, tile_ids, row[:, None]], axis=1).astype(np.float32)


def experts(nc, xn_dram, router_dram, weights, consts, out):
    T, D = xn_dram.shape
    ROWS, S = router_dram.shape
    E, CHUNKS, _, _ = weights.shape
    CAP = T // E
    TILES = T // P
    TB = S // P
    B = ROWS // E
    CT = D // P
    H = 1024
    HALF = CAP // 2
    HT = H // P
    CAPT = CAP // P
    HTT = CAPT // 2
    PARTS = 5
    GROUP = TILES // 4
    BITS = 31

    with ExitStack() as ctx:
        def sb(name, shape, dt=F32):
            return ctx.enter_context(nc.sbuf_tensor(name, shape, dt))

        def sem(name):
            return ctx.enter_context(nc.semaphore(name))

        tables = sb("tables", [P, 4 * P + TILES + 1])
        same, before, ident, numbers = (tables[:, i * P:(i + 1) * P] for i in range(4))
        tile_ids = tables[:, 4 * P:4 * P + TILES]
        row_id = tables[:, 4 * P + TILES:4 * P + TILES + 1]
        numbers_b = sb("numbers_b", [P, P], BF16)
        loT = sb("loT", [P, B, TB, E], BF16)
        hiT = sb("hiT", [P, B, TB, E], BF16)
        wT = [sb(f"wT{i}", [P, B, TB, E], BF16) for i in range(3)]

        with ExitStack() as rctx:
            def rsb(name, shape, dt=F32):
                return rctx.enter_context(nc.sbuf_tensor(name, shape, dt))

            sc = rsb("sc", [P, S])
            work = rsb("work", [P, S])
            ones = rsb("r_ones", [P, S])
            sel = rsb("sel", [P, S])
            eq = rsb("eq", [P, S])
            rank = rsb("rank", [P, S])
            ex = rsb("ex", [P, S])
            place_i = rsb("place_i", [P, S], I32)
            lo_i = rsb("lo_i", [P, S], I32)
            hi_i = rsb("hi_i", [P, S], I32)
            lo = rsb("lo", [P, S])
            hi = rsb("hi", [P, S])
            w = rsb("w", [P, S])
            wrest = rsb("wrest", [P, TB, P])
            thr = rsb("thr", [P, 1], I32)
            cand = rsb("cand", [P, 1], I32)
            step = rsb("step", [P, 1], I32)
            bit = rsb("bit", [P, 1], I32)
            bit_f = rsb("bit_f", [P, 1])
            count = rsb("count", [P, 1])
            stat = rsb("stat", [P, 12])
            top = rsb("top", [P, P])
            top_row = rsb("top_row", [1, 2, P])
            ps_tot = rctx.enter_context(nc.psum_tensor("ps_tot", [P, 512], F32))
            ps_a = rctx.enter_context(nc.psum_tensor("ps_a", [P, 512], F32))
            ps_t = [rctx.enter_context(nc.psum_tensor(f"ps_t{i}", [P, TB, P], F32)) for i in range(3)]

            def rsem(name):
                return rctx.enter_context(nc.semaphore(name))

            r_in = rsem("r_in")
            link_s = rsem("link_s")
            cand_done, count_done = rsem("cand_done"), rsem("count_done")
            total_done, step_done = rsem("total_done"), rsem("step_done")
            thr_done = rsem("thr_done")
            bit_done = rsem("bit_done")
            asks, answers = rsem("asks"), rsem("answers")
            max_ready, ex_done = rsem("max_ready"), rsem("ex_done")
            lists_ready, listsT = rsem("lists_ready"), rsem("listsT")

            block = rctx.enter_context(nc.Block())

            @block.sync
            def _(sp):
                sp.dma_start(sc[:, :], router_dram).then_inc(r_in, 16)
                sp.dma_start(tables[:, :], consts).then_inc(r_in, 16)

            @block.tensor
            def _(pe):
                pe.wait_ge(r_in, 32)
                pe.wait_ge(count_done, 1)
                nc.tensor.matmul(ps_tot[:, 0:1], same, count[:, :], start=True, stop=True).then_inc(total_done, 1)
                with pe.Fori(1, BITS + 1) as i:
                    pe.wait_ge(count_done, i + 1)
                    nc.tensor.matmul(ps_tot[:, 0:1], same, count[:, :], start=True, stop=True).then_inc(total_done, 1)
                pe.wait_ge(asks, 1)
                nc.tensor.matmul(ps_a[:, 0:1], same, stat[:, 0:1], start=True, stop=True)
                nc.tensor.matmul(ps_a[:, 1:2], before, stat[:, 1:2], start=True, stop=True).then_inc(answers, 1)
                pe.wait_ge(asks, 2)
                nc.tensor.matmul(ps_a[:, 0:1], before, stat[:, 2:3], start=True, stop=True)
                nc.tensor.matmul(ps_a[:, P:2 * P], top[:, :], ident, is_transpose=True, start=True, stop=True).then_inc(answers, 1)
                pe.wait_ge(asks, 3)
                nc.tensor.matmul(ps_a[:, 0:1], top_row[0:1, 1, :], ones[0:1, 0:1], start=True, stop=True).then_inc(answers, 1)
                pe.wait_ge(asks, 4)
                nc.tensor.matmul(ps_a[:, 0:1], same, stat[:, 5:6], start=True, stop=True).then_inc(answers, 1)
                for k, src in enumerate((lo, hi, w)):
                    pe.wait_ge(lists_ready, k + 1)
                    for c in range(TB):
                        last = nc.tensor.matmul(ps_t[k][:, c, :], src[:, c * P:(c + 1) * P], ident, is_transpose=True, start=True, stop=True)
                    last.then_inc(listsT, 1)

            @block.scalar
            def _(act):
                act.wait_ge(max_ready, 1)
                nc.scalar.activation(ex[:, :], sc[:, :], ACT.Exp, bias=stat[:, 4:5]).then_inc(ex_done, 1)

            @block.vector
            def _(dve):
                steps = [0]

                def link(ins):
                    steps[0] += 1
                    ins.then_inc(link_s, 1)
                    dve.wait_ge(link_s, steps[0])

                nc.vector.memset(ones[:, :], 1.0)
                nc.vector.memset(top[:, :], 0.0)
                nc.vector.memset(bit[:, :], 1 << (BITS - 1))
                link(nc.vector.memset(bit_f[:, :], float(1 << (BITS - 1))))
                dve.wait_ge(r_in, 32)
                nc.vector.tensor_scalar(out=work[:, :], in0=sc[:, :], scalar1=0.0, scalar2=0.0, op0=ALU.is_ge, op1=ALU.add,
                                        accum_out=count[:, :]).then_inc(count_done, 1)
                dve.wait_ge(total_done, 1)
                nc.vector.tensor_scalar(out=thr[:, :], in0=ps_tot[:, 0:1], scalar1=float(CAP), scalar2=-1.0, op0=ALU.is_lt,
                                        op1=ALU.mult).then_inc(thr_done, 1)
                with dve.Fori(1, BITS + 1) as i:
                    dve.wait_ge(thr_done, i)
                    nc.vector.tensor_tensor(out=cand[:, :], in0=thr[:, :], in1=bit[:, :], op=ALU.bitwise_xor).then_inc(cand_done, 1)
                    dve.wait_ge(cand_done, i)
                    nc.vector.tensor_scalar(out=work[:, :], in0=sc[:, :], scalar1=cand[:, :].bitcast(F32), scalar2=0.0, op0=ALU.is_ge,
                                            op1=ALU.add, accum_out=count[:, :]).then_inc(count_done, 1)
                    nc.vector.tensor_scalar(out=bit[:, :], in0=bit[:, :], scalar1=1, scalar2=None, op0=ALU.logical_shift_right).then_inc(bit_done, 1)
                    dve.wait_ge(total_done, i + 1)
                    nc.vector.tensor_scalar(out=step[:, :], in0=ps_tot[:, 0:1], scalar1=float(CAP), scalar2=bit_f[:, :], op0=ALU.is_ge,
                                            op1=ALU.mult).then_inc(step_done, 1)
                    dve.wait_ge(step_done, i)
                    dve.wait_ge(bit_done, 2 * i - 1)
                    nc.vector.tensor_scalar(out=bit_f[:, :], in0=bit_f[:, :], scalar1=0.5, scalar2=None, op0=ALU.mult).then_inc(bit_done, 1)
                    nc.vector.tensor_tensor(out=thr[:, :], in0=thr[:, :], in1=step[:, :], op=ALU.bitwise_xor).then_inc(thr_done, 1)
                dve.wait_ge(thr_done, BITS + 1)
                limit = thr[:, :].bitcast(F32)
                nc.vector.tensor_scalar(out=sel[:, :], in0=sc[:, :], scalar1=limit, scalar2=0.0, op0=ALU.is_gt, op1=ALU.add,
                                        accum_out=stat[:, 0:1])
                link(nc.vector.tensor_scalar(out=eq[:, :], in0=sc[:, :], scalar1=limit, scalar2=0.0, op0=ALU.is_equal, op1=ALU.add,
                                             accum_out=stat[:, 1:2]))
                nc.vector.tensor_tensor_scan(out=rank[:, :], data0=ones[:, :], data1=eq[:, :], initial=0.0, op0=ALU.mult,
                                             op1=ALU.add).then_inc(asks, 1)
                dve.wait_ge(asks, 1)
                dve.wait_ge(answers, 1)
                link(nc.vector.tensor_scalar(out=stat[:, 3:4], in0=ps_a[:, 0:1], scalar1=-1.0, scalar2=float(CAP), op0=ALU.mult, op1=ALU.add))
                link(nc.vector.tensor_tensor(out=stat[:, 3:4], in0=stat[:, 3:4], in1=ps_a[:, 1:2], op=ALU.subtract))
                link(nc.vector.scalar_tensor_tensor(out=eq[:, :], in0=rank[:, :], scalar=stat[:, 3:4], in1=eq[:, :], op0=ALU.is_le, op1=ALU.mult))
                link(nc.vector.tensor_tensor(out=sel[:, :], in0=sel[:, :], in1=eq[:, :], op=ALU.add))
                link(nc.vector.tensor_tensor_scan(out=rank[:, :], data0=ones[:, :], data1=sel[:, :], initial=0.0, op0=ALU.mult, op1=ALU.add))
                nc.vector.tensor_copy(stat[:, 2:3], rank[:, S - 1:S])
                link(nc.vector.tensor_reduce(out=top[:, 0:1], in_=sc[:, :], axis=AX_X, op=ALU.max))
                nc.vector.tensor_scalar(out=work[:, :], in0=sel[:, :], scalar1=-512.0, scalar2=512.0, op0=ALU.mult, op1=ALU.add).then_inc(asks, 1)
                dve.wait_ge(asks, 2)
                dve.wait_ge(answers, 2)
                link(nc.vector.tensor_copy(stat[:, 6:7], ps_a[:, 0:1]))
                link(nc.vector.tensor_scalar(out=place_i[:, :], in0=rank[:, :], scalar1=stat[:, 6:7], scalar2=-1.0, op0=ALU.add, op1=ALU.add))
                link(nc.vector.tensor_reduce(out=top_row[0:1, 0, 0:E], in_=ps_a[0:1, P:2 * P].rearrange("o (b e) -> o e b", e=E), axis=AX_X, op=ALU.max))
                nc.vector.tensor_copy(top_row[0:1, 1, :].rearrange("o (b e) -> o b e", e=E),
                                      top_row[0:1, 0:1, 0:E].broadcast_to([1, B, E])).then_inc(asks, 1)
                dve.wait_ge(asks, 3)
                dve.wait_ge(answers, 3)
                nc.vector.tensor_scalar(out=stat[:, 4:5], in0=ps_a[:, 0:1], scalar1=-1.0, scalar2=None, op0=ALU.mult).then_inc(max_ready, 1)
                link(nc.vector.tensor_scalar(out=lo_i[:, :], in0=place_i[:, :], scalar1=P - 1, scalar2=None, op0=ALU.bitwise_and))
                link(nc.vector.tensor_scalar(out=hi_i[:, :], in0=place_i[:, :], scalar1=7, scalar2=None, op0=ALU.arith_shift_right))
                nc.vector.tensor_tensor(out=lo[:, :], in0=lo_i[:, :], in1=work[:, :], op=ALU.add).then_inc(lists_ready, 1)
                nc.vector.tensor_copy(hi[:, :], hi_i[:, :]).then_inc(lists_ready, 1)
                dve.wait_ge(ex_done, 1)
                link(nc.vector.tensor_tensor(out=ex[:, :], in0=ex[:, :], in1=sel[:, :], op=ALU.mult))
                nc.vector.tensor_reduce(out=stat[:, 5:6], in_=ex[:, :], axis=AX_X, op=ALU.add).then_inc(asks, 1)
                dve.wait_ge(answers, 4)
                link(nc.vector.reciprocal(stat[:, 7:8], ps_a[:, 0:1]))
                dve.wait_ge(lists_ready, 2)
                nc.vector.tensor_scalar(out=w[:, :], in0=ex[:, :], scalar1=stat[:, 7:8], scalar2=None, op0=ALU.mult).then_inc(lists_ready, 1)
                nc.vector.tensor_copy(numbers_b[:, :], numbers)

                def by_token(t):
                    return t.rearrange("p b c e -> p c b e")

                dve.wait_ge(listsT, 3)
                nc.vector.tensor_copy(by_token(loT[:, :, :, :]), ps_t[0][:, :, :].rearrange("p c (b e) -> p c b e", e=E))
                nc.vector.tensor_copy(by_token(hiT[:, :, :, :]), ps_t[1][:, :, :].rearrange("p c (b e) -> p c b e", e=E))
                rest = wrest[:, :, :].rearrange("p c (b e) -> p c b e", e=E)
                link(nc.vector.tensor_copy(rest, ps_t[2][:, :, :].rearrange("p c (b e) -> p c b e", e=E)))
                for i in range(3):
                    link(nc.vector.tensor_copy(by_token(wT[i][:, :, :, :]), rest))
                    if i < 2:
                        link(nc.vector.tensor_tensor(out=rest, in0=rest, in1=by_token(wT[i][:, :, :, :]), op=ALU.subtract))

        w_stage = sb("w_stage", [P, 2, 4 * 512])
        w_hi = [sb(f"ew{k}_hi", [P, 4, 512], F32R) for k in range(CHUNKS)]
        w_lo = [sb(f"ew{k}_lo", [P, 4, 512], F32R) for k in range(CHUNKS)]
        xg = sb("xg", [P, HTT, D])
        xT_hi = sb("exT_hi", [P, CT, HALF], F32R)
        xT_lo = sb("exT_lo", [P, CT, HALF], F32R)
        silu = sb("silu", [P, 2, HALF])
        g_f = sb("g_f", [P, 2, HALF])
        g_hi = sb("g_hi", [P, HT, HALF], F32R)
        g_lo = sb("g_lo", [P, HT, HALF], F32R)
        y = sb("y", [P, HTT, D])
        onehot = sb("onehot", [P, 2, GROUP, P], BF16)
        has_hi = sb("has_hi", [P, TILES, CAPT], BF16)
        payload = sb("payload", [P, TILES, PARTS, CAPT], BF16)
        lists = sb("lists", [P, PARTS, CAPT])
        idx_in = sb("idx_in", [P, CAPT], U32)
        idx_out = sb("idx_out", [P, CAPT], U32)
        w_next = sb("w_next", [P, CAPT])
        w_now = sb("w_now", [P, CAPT])
        w_sum = sb("w_sum", [P, CAPT])

        def psum(name, shape):
            return ctx.enter_context(nc.psum_tensor(name, shape, F32))

        ps_h = [[psum(f"ps_h{i}{j}", [P, HALF]) for j in range(2)] for i in range(2)]
        ps_y = [psum(f"ps_y{i}", [P, D]) for i in range(2)]
        ps_x = psum("ps_x", [P, CT, P])
        ps_l = psum("ps_l", [P, 512])

        w_in = [sem(f"ew_in{i}") for i in range(2)]
        w_hi_done, w_lo_done = sem("ew_hi_done"), sem("ew_lo_done")
        has_done = sem("has_done")
        payload_done = sem("payload_done")
        onehot_done = sem("onehot_done")
        list_step = sem("list_step")
        lists_done = sem("lists_done")
        idx_done = sem("idx_done")
        wsum_done = sem("wsum_done")
        wnext_done = sem("wnext_done")
        now_done = sem("now_done")
        gathered = [sem(f"gathered{i}") for i in range(HTT)]
        xT_done = sem("xT_done")
        xThi_done, xTlo_done = sem("xThi_done"), sem("xTlo_done")
        h_done = sem("h_done")
        silu_done, g_f_done = sem("silu_done"), sem("g_f_done")
        g_hi_done, g_lo_done = sem("g_hi_done"), sem("g_lo_done")
        y_done = sem("y_done")
        y_ready = sem("y_ready")
        scattered = sem("scattered")
        pool_waited = sem("pool_waited")

        block = ctx.enter_context(nc.Block())

        def over_experts(eng, body):
            body(0, True, False)
            with eng.Fori(1, E - 1) as e:
                body(e, False, False)
            body(E - 1, False, True)

        def need(eng, s, value):
            if not (isinstance(value, int) and value <= 0):
                eng.wait_ge(s, value)

        @block.sync
        def _(sp):
            def load(e, k):
                sp.dma_start(w_stage[:, k % 2, :], weights[bass.ds(e, 1), k].rearrange("o p n -> p (o n)")).then_inc(w_in[k % 2], 16)

            for k in range(CHUNKS):
                if k >= 2:
                    sp.wait_ge(w_lo_done, k - 1)
                load(0, k)

            def body(e, first, last):
                if not last:
                    for k in range(CHUNKS):
                        sp.wait_ge(w_lo_done, CHUNKS * (e + 1) + k - 1)
                        load(e + 1, k)

            over_experts(sp, body)

        @block.tensor
        def _(pe):
            def transpose_tile(e, i):
                n = CAPT * e + i
                pe.wait_ge(gathered[i % HTT], 16 * (2 * e + i // HTT + 1))
                need(pe, xTlo_done, n)
                for c in range(CT):
                    last = nc.tensor.matmul(ps_x[:, c, :], xg[:, i % HTT, c * P:(c + 1) * P], ident, is_transpose=True, start=True, stop=True)
                last.then_inc(xT_done, 1)

            def hidden(e, half, ht):
                n = 2 * HT * e + HT * half + ht
                if half == 0 and ht % 4 == 0:
                    pe.wait_ge(w_lo_done, CHUNKS * e + (2 if ht == 0 else 4))
                if ht == 0:
                    pe.wait_ge(xTlo_done, CAPT * e + HTT * (half + 1))
                need(pe, g_f_done, n - 1)
                f = slice((ht % 4) * P, (ht % 4 + 1) * P)
                for j in range(2):
                    k = 2 * (ht // 4) + j
                    for c in range(CT):
                        for i, (l, r) in enumerate(((w_hi[k], xT_hi), (w_hi[k], xT_lo), (w_lo[k], xT_hi))):
                            last = nc.tensor.matmul(ps_h[ht % 2][j][:, :], l[:, c, f], r[:, c, :], start=(c == 0 and i == 0),
                                                    stop=(c == CT - 1 and i == 2))
                last.then_inc(h_done, 1)

            def output(e, half, t):
                n = CAPT * e + HTT * half + t
                if half == 0 and t == 0:
                    pe.wait_ge(w_lo_done, CHUNKS * e + CHUNKS)
                if t == 0:
                    pe.wait_ge(g_lo_done, 2 * HT * e + HT * (half + 1))
                need(pe, y_ready, n - 1)
                s = slice(t * P, (t + 1) * P)
                for ht in range(HT):
                    k, f = 4 + ht // 4, ht % 4
                    for i, (l, r) in enumerate(((g_hi, w_hi[k]), (g_hi, w_lo[k]), (g_lo, w_hi[k]))):
                        last = nc.tensor.matmul(ps_y[t % 2][:, :], l[:, ht, s], r[:, f, :], start=(ht == 0 and i == 0),
                                                stop=(ht == HT - 1 and i == 2))
                last.then_inc(y_done, 1)

            def list_part(e, q):
                pe.wait_ge(onehot_done, 4 * e + q + 1)
                if q == 0:
                    pe.wait_ge(payload_done, 5 * e + 5)
                    need(pe, lists_done, e)
                for t in range(GROUP):
                    n = q * GROUP + t
                    last = nc.tensor.matmul(ps_l[:, 0:PARTS * CAPT], onehot[:, q % 2, t, :],
                                            payload[:, n, :, :].rearrange("p k j -> p (k j)"), start=(n == 0), stop=(n == TILES - 1))
                last.then_inc(list_step, 1)

            for q in range(4):
                list_part(0, q)
            for i in range(HTT):
                transpose_tile(0, i)

            def body(e, first, last):
                for half in range(2):
                    for ht in range(HT):
                        hidden(e, half, ht)
                        if half == 0 and not last and ht in (2, 3, 4, 5):
                            list_part(e + 1, ht - 2)
                    for t in range(HTT):
                        output(e, half, t)
                        if half == 0:
                            transpose_tile(e, HTT + t)
                        elif not last:
                            transpose_tile(e + 1, t)

            over_experts(pe, body)

        @block.scalar
        def _(act):
            def split_w(e, k):
                act.wait_ge(w_in[k % 2], 16 * (CHUNKS // 2 * e + k // 2 + 1))
                if k < 4:
                    need(act, h_done, 2 * HT * e - HT + (4 if k < 2 else 8) if not (isinstance(e, int) and e == 0) else 0)
                else:
                    need(act, y_done, CAPT * e)
                nc.scalar.activation(w_hi[k][:, :, :], w_stage[:, k % 2, :].rearrange("p (c n) -> p c n", c=4), ACT.Copy).then_inc(w_hi_done, 1)

            def tile_hi(e, i):
                s = slice((i % HTT) * P, (i % HTT + 1) * P)
                act.wait_ge(xT_done, CAPT * e + i + 1)
                nc.scalar.activation(xT_hi[:, :, s], ps_x[:, :, :], ACT.Copy).then_inc(xThi_done, 1)

            def gate(e, half, ht):
                n = 2 * HT * e + HT * half + ht
                act.wait_ge(h_done, n + 1)
                need(act, g_f_done, n - 1)
                nc.scalar.activation(silu[:, ht % 2, :], ps_h[ht % 2][0][:, :], ACT.Silu).then_inc(silu_done, 1)

            def hidden_hi(e, half, ht):
                n = 2 * HT * e + HT * half + ht
                act.wait_ge(g_f_done, n + 1)
                nc.scalar.activation(g_hi[:, ht, :], g_f[:, ht % 2, :], ACT.Copy).then_inc(g_hi_done, 1)

            for k in range(4):
                split_w(0, k)
            for i in range(HTT):
                tile_hi(0, i)

            def body(e, first, last):
                for half in range(2):
                    for ht in range(HT):
                        gate(e, half, ht)
                        if ht == 0:
                            need(act, y_done, CAPT * e + HTT * half)
                        hidden_hi(e, half, ht)
                        if half == 0 and ht in (1, 2):
                            split_w(e, 3 + ht)
                        if half == 1 and ht in (4, 5) and not last:
                            split_w(e + 1, ht - 4)
                    for t in range(HTT):
                        if half == 0:
                            tile_hi(e, HTT + t)
                        elif not last:
                            if t in (0, 1):
                                split_w(e + 1, 2 + t)
                            tile_hi(e + 1, t)

            over_experts(act, body)

        @block.vector
        def _(dve):
            def split_w(e, k):
                dve.wait_ge(w_hi_done, CHUNKS * e + k + 1)
                nc.vector.tensor_tensor(out=w_lo[k][:, :, :], in0=w_stage[:, k % 2, :].rearrange("p (c n) -> p c n", c=4),
                                        in1=w_hi[k][:, :, :].bitcast(F32), op=ALU.subtract).then_inc(w_lo_done, 1)

            def tile_lo(e, i):
                s = slice((i % HTT) * P, (i % HTT + 1) * P)
                dve.wait_ge(xThi_done, CAPT * e + i + 1)
                nc.vector.tensor_tensor(out=xT_lo[:, :, s], in0=ps_x[:, :, :], in1=xT_hi[:, :, s].bitcast(F32),
                                        op=ALU.subtract).then_inc(xTlo_done, 1)

            def gated(e, half, ht):
                n = 2 * HT * e + HT * half + ht
                dve.wait_ge(silu_done, n + 1)
                need(dve, g_hi_done, n - 1)
                nc.vector.tensor_tensor(out=g_f[:, ht % 2, :], in0=ps_h[ht % 2][1][:, :], in1=silu[:, ht % 2, :], op=ALU.mult).then_inc(g_f_done, 1)

            def hidden_lo(e, half, ht):
                n = 2 * HT * e + HT * half + ht
                dve.wait_ge(g_hi_done, n + 1)
                nc.vector.tensor_tensor(out=g_lo[:, ht, :], in0=g_f[:, ht % 2, :], in1=g_hi[:, ht, :].bitcast(F32),
                                        op=ALU.subtract).then_inc(g_lo_done, 1)

            def weigh(e, half, t):
                n = CAPT * e + HTT * half + t
                dve.wait_ge(y_done, n + 1)
                need(dve, scattered, 16 * (n - HTT + 1))
                if half == 0 and t == 0:
                    dve.wait_ge(now_done, 2 * e + 2)
                c = HTT * half + t
                nc.vector.tensor_scalar(out=y[:, t, :], in0=ps_y[t % 2][:, :], scalar1=w_now[:, c:c + 1], scalar2=None,
                                        op0=ALU.mult).then_inc(y_ready, 1)

            def make_payload(e):
                def over(t):
                    return t.rearrange("p b c e -> p (b c) e")[:, :, bass.ds(e, 1)].broadcast_to([P, TILES, CAPT])

                need(dve, list_step, 4 * e)
                nc.vector.tensor_tensor(out=has_hi[:, :, :], in0=over(hiT[:, :, :, :]),
                                        in1=numbers_b[:, 0:CAPT].rearrange("p (o j) -> p o j", o=1).broadcast_to([P, TILES, CAPT]),
                                        op=ALU.is_equal).then_inc(has_done, 1)
                dve.wait_ge(has_done, e + 1)
                ids = tile_ids.rearrange("p (n o) -> p n o", o=1).broadcast_to([P, TILES, CAPT])
                nc.vector.tensor_tensor(out=payload[:, :, 0, :], in0=has_hi[:, :, :], in1=ids, op=ALU.mult).then_inc(payload_done, 1)
                nc.vector.tensor_scalar(out=payload[:, :, 1, :], in0=has_hi[:, :, :], scalar1=row_id, scalar2=None, op0=ALU.mult).then_inc(payload_done, 1)
                for i in range(3):
                    nc.vector.tensor_tensor(out=payload[:, :, 2 + i, :], in0=has_hi[:, :, :], in1=over(wT[i][:, :, :, :]), op=ALU.mult).then_inc(payload_done, 1)

            def make_onehot(e, q):
                need(dve, list_step, 4 * e + q - 1)
                lo_q = loT[:, :, :, :].rearrange("p b c e -> p (b c) e")[:, q * GROUP:(q + 1) * GROUP, bass.ds(e, 1)].broadcast_to([P, GROUP, P])
                nc.vector.tensor_tensor(out=onehot[:, q % 2, :, :], in0=lo_q,
                                        in1=numbers_b[:, :].rearrange("p (o j) -> p o j", o=1).broadcast_to([P, GROUP, P]),
                                        op=ALU.is_equal).then_inc(onehot_done, 1)

            def read_lists(e):
                dve.wait_ge(list_step, 4 * e + 4)
                nc.vector.tensor_copy(lists[:, :, :], ps_l[:, 0:PARTS * CAPT].rearrange("p (k j) -> p k j", k=PARTS)).then_inc(lists_done, 1)
                dve.wait_ge(lists_done, e + 1)
                for i in range(HTT):
                    need(dve, gathered[i], 32 * e)
                need(dve, now_done, 2 * e)
                nc.vector.scalar_tensor_tensor(out=idx_in[:, :], in0=lists[:, 0, :], scalar=float(P), in1=lists[:, 1, :], op0=ALU.mult,
                                               op1=ALU.add).then_inc(idx_done, 1)
                nc.vector.tensor_tensor(out=w_sum[:, :], in0=lists[:, 2, :], in1=lists[:, 3, :], op=ALU.add).then_inc(wsum_done, 1)
                dve.wait_ge(wsum_done, e + 1)
                nc.vector.tensor_tensor(out=w_next[:, :], in0=w_sum[:, :], in1=lists[:, 4, :], op=ALU.add).then_inc(wnext_done, 1)

            def take_lists(e):
                dve.wait_ge(wnext_done, e + 1)
                need(dve, scattered, 16 * CAPT * e)
                nc.vector.tensor_copy(idx_out[:, :], idx_in[:, :]).then_inc(now_done, 1)
                nc.vector.tensor_copy(w_now[:, :], w_next[:, :]).then_inc(now_done, 1)

            make_payload(0)
            for q in range(4):
                make_onehot(0, q)
            read_lists(0)
            for k in range(4):
                split_w(0, k)
            for i in range(HTT):
                tile_lo(0, i)

            def body(e, first, last):
                for half in range(2):
                    for ht in range(HT):
                        gated(e, half, ht)
                        hidden_lo(e, half, ht)
                        if half == 0:
                            if ht == 0:
                                take_lists(e)
                            if ht in (1, 2):
                                split_w(e, 3 + ht)
                            if not last:
                                if ht == 0:
                                    make_payload(e + 1)
                                    make_onehot(e + 1, 0)
                                if ht in (1, 2, 3):
                                    make_onehot(e + 1, ht)
                                if ht == 6:
                                    read_lists(e + 1)
                        elif ht in (4, 5) and not last:
                            split_w(e + 1, ht - 4)
                    for t in range(HTT):
                        weigh(e, half, t)
                        if half == 0:
                            tile_lo(e, HTT + t)
                        elif not last:
                            if t in (0, 1):
                                split_w(e + 1, 2 + t)
                            tile_lo(e + 1, t)

            over_experts(dve, body)

        @block.gpsimd
        def _(pool):
            def gather(e, i):
                pool.wait_ge(idx_done, e + 1)
                need(pool, xT_done, CAPT * e + i - HTT + 1)
                pool.sem_inc(pool_waited, 1)
                pool.indirect_dma_start(out=xg[:, i % HTT, :], out_offset=None, in_=xn_dram,
                                        in_offset=bass.IndirectOffsetOnAxis(ap=idx_in[:, i:i + 1], axis=0)).then_inc(gathered[i % HTT], 16)

            def scatter(e, i):
                n = CAPT * e + i
                pool.wait_ge(now_done, 2 * e + 2)
                need(pool, scattered, 16 * n)
                pool.wait_ge(y_ready, n + 1)
                pool.sem_inc(pool_waited, 1)
                pool.indirect_dma_start(out=out, out_offset=bass.IndirectOffsetOnAxis(ap=idx_out[:, i:i + 1], axis=0), in_=y[:, i % HTT, :],
                                        in_offset=None, compute_op=ALU.add).then_inc(scattered, 16)

            for i in range(HTT):
                gather(0, i)

            def body(e, first, last):
                for i in range(HTT):
                    gather(e, HTT + i)
                for i in range(HTT):
                    scatter(e, i)
                if not last:
                    for i in range(HTT):
                        gather(e + 1, i)
                for i in range(HTT):
                    scatter(e, HTT + i)

            over_experts(pool, body)
            pool.wait_ge(scattered, 16 * CAPT * E)


def program(nc, x, ctx, mask, wq, wk, wv, wo, bq, bk, bv, bo, wg, weights, consts, out):
    B, S, D = x.shape
    E = wg.shape[2]
    xn = nc.dram_tensor("normed", [B * S, D], F32, kind="Internal").ap()
    router = nc.dram_tensor("router", [B * E, S], F32, kind="Internal").ap()
    q_parts, k_parts = (nc.dram_tensor(n, [D // P, P, 2, S], F32, kind="Internal").ap() for n in ("q_parts", "k_parts"))
    attention(nc, x, ctx, mask, {"q": wq, "k": wk, "v": wv, "o": wo}, bq, bk, bv, bo, wg, out,
              xn.rearrange("(b s) d -> b s d", b=B), router.rearrange("(b e) s -> b e s", b=B), q_parts, k_parts)
    experts(nc, xn, router, weights, consts, out.rearrange("b s d -> (b s) d"))


def kernel(x, ctx_1024, mask_Bx1x1xS2_if1, L0_xattn_wq, L0_xattn_bq, L0_xattn_wk, L0_xattn_bk, L0_xattn_wv, L0_xattn_bv,
           L0_xattn_wo, L0_xattn_bo, L0_ffn_Wg, L0_ffn_W1, L0_ffn_W2, L0_ffn_W3):
    from concourse import bacc
    from concourse.bass_utils import run_bass_kernel_spmd

    def host(a):
        return np.asarray(a)

    def by_feature(a):
        return host(a).reshape(-1, P).T

    def chunks_in(w):
        e, h, c = w.shape
        return w.reshape(e, h // 512, 512, c // P, P).transpose(0, 1, 4, 3, 2).reshape(e, h // 512, P, -1)

    def chunks_out(w):
        e, c, h = w.shape
        return w.reshape(e, c, h // 512, 4, P).transpose(0, 2, 4, 3, 1).reshape(e, h // 512, P, -1)

    x = host(x)
    B, S, D = x.shape
    w1, w3, w2 = chunks_in(host(L0_ffn_W1)), chunks_in(host(L0_ffn_W3)), chunks_out(host(L0_ffn_W2))
    wg = host(L0_ffn_Wg)
    E = wg.shape[0]
    arrays = {
        "x": x,
        "ctx": host(ctx_1024).transpose(0, 2, 1),
        "mask": host(mask_Bx1x1xS2_if1).reshape(B, S),
        "wq": host(L0_xattn_wq).T,
        "wk": host(L0_xattn_wk).T,
        "wv": host(L0_xattn_wv).T,
        "wo": host(L0_xattn_wo).T,
        "bq": by_feature(L0_xattn_bq),
        "bk": by_feature(L0_xattn_bk),
        "bv": by_feature(L0_xattn_bv),
        "bo": host(L0_xattn_bo),
        "wg": wg.T.reshape(D // P, P, E).transpose(1, 0, 2),
        "weights": np.stack([w1[:, 0], w3[:, 0], w1[:, 1], w3[:, 1], w2[:, 0], w2[:, 1]], axis=1),
        "consts": route_constants(B, E, S // P),
    }
    arrays = {f"in_{n}": np.ascontiguousarray(a) for n, a in arrays.items()}
    nc = bacc.Bacc("TRN2", target_bir_lowering=False, num_devices=1)
    args = [nc.dram_tensor(n, a.shape, mybir.dt.from_np(a.dtype), kind="ExternalInput").ap() for n, a in arrays.items()]
    out = nc.dram_tensor("out", x.shape, F32, kind="ExternalOutput").ap()
    program(nc, *args, out)
    return run_bass_kernel_spmd(nc, [arrays], core_ids=[0]).results[0]["out"]
```

```python
from contextlib import ExitStack

import numpy as np

import concourse.bass as bass
from concourse import mybir

F32 = mybir.dt.float32
F32R = mybir.dt.float32r
BF16 = mybir.dt.bfloat16
I32 = mybir.dt.int32
U32 = mybir.dt.uint32
ALU = mybir.AluOpType
ACT = mybir.ActivationFunctionType
AX_X = mybir.AxisListType.X

P = 128
EPS = 1e-5
MASKED = -1e9
POOL_INIT = 5


def high_part(value):
    bits = np.float32(value).view(np.uint32) & np.uint32(0xFFFFF000)
    return float(bits.view(np.float32))


def over_batches(eng, batches, body):
    body(0, True, False)
    with eng.Fori(1, batches - 1) as b:
        body(b, False, False)
    body(batches - 1, False, True)


def attention(nc, x, ctxT, mask, wT, bq, bk, bv, bo, wgT, out, xn_dram, router_dram, q_parts, k_parts):
    B, S, D = x.shape
    H, DK = 16, 32
    CT = D // P
    KT = S // P
    HG = P // DK
    NG = H // HG
    QW = S // 2
    QT = QW // P
    UNITS = NG * 2
    E = wgT.shape[2]
    SCALE = float(DK) ** -0.5
    MASK_HI = high_part(MASKED / SCALE)
    MASK_LO = float(np.float32(MASKED / SCALE)) - MASK_HI
    ROWS_MASK = 3 * DK
    ROWS_MAX = ROWS_MASK + 2
    ROWS = ROWS_MAX + 2
    MX_ROWS = 16 * 2

    with ExitStack() as ctx:
        def sb(name, shape, dt=F32):
            return ctx.enter_context(nc.sbuf_tensor(name, shape, dt))

        def psum(name, shape):
            return ctx.enter_context(nc.psum_tensor(name, shape, F32))

        def sem(name):
            return ctx.enter_context(nc.semaphore(name))

        w_hi = {n: sb(f"w{n}_hi", [P, CT, D], F32R) for n in "qkvo"}
        w_lo = {n: sb(f"w{n}_lo", [P, CT, D], F32R) for n in "qkvo"}
        tok = sb("tok", [P, KT, D])
        tok2 = sb("tok2", [P, KT, D])
        ctx_hi = sb("ctx_hi", [P, CT, S], F32R)
        ctx_lo = sb("ctx_lo", [P, CT, S], F32R)
        xT_hi = sb("xT_hi", [P, CT, S], F32R)
        xT_lo = sb("xT_lo", [P, CT, S], F32R)
        v = sb("v", [P, KT, D])
        qs = sb("qs", [P, 2, HG, S], F32R)
        ks = sb("ks", [P, 2, HG, S], F32R)
        q_st = sb("q_st", [P, 2, S], F32R)
        k_st = sb("k_st", [P, 2, S], F32R)
        ctx_f = sb("ctx_f", [P, 2, S])
        xnT = ctx_f[:, 1, :]
        probs = sb("probs", [P, KT, HG, QW])
        psumk = sb("psumk", [P, HG, QW])
        at_f = sb("at_f", [P, QW])
        at_hi = sb("at_hi", [P, NG, S], F32R)
        at_lo = sb("at_lo", [P, NG, S], F32R)
        keep = sb("keep", [P, S])
        bo_row = sb("bo_row", [P, D])
        ident = sb("ident", [P, P])
        mx = sb("mx", [P, QT, HG])
        mx_parts = sb("mx_parts", [32 + HG, QW], F32R)
        mx_hi, mx_lo = mx_parts[0:HG, :], mx_parts[32:32 + HG, :]
        rscore = sb("rscore", [E, P])
        wg = sb("wg", [P, CT, E])
        ones = sb("ones", [P, DK])
        b_q, b_k, b_v = (sb(f"b_{n}", [P, NG]) for n in "qkv")
        masked = sb("masked", [P, 1])
        stats = sb("stats", [P, 2, KT, 6])
        mv = sb("mv", [P, 2, KT, 2])
        rstd = sb("rstd", [P, 2, KT])
        half = sb("half", [P, KT])
        eps = sb("eps", [P, KT])
        w_f = probs[:, :, :, :].rearrange("p k h q -> p (k h q)").rearrange("p (s c d) -> p s c d", s=2, d=D)

        ps_max = psum("ps_max", [P, 2, S])
        ps_exp = psum("ps_exp", [P, HG, QW])
        ps_av = [psum(f"ps_av{i}", [P, 2, QW]) for i in range(2)]
        ps_job = [psum(f"ps_job{i}", [P, 512]) for i in range(2)]

        consts_in = sem("consts_in")
        w_in = [sem(f"w_in{i}") for i in range(2)]
        w_hi_done = sem("w_hi_done")
        w_lo_done = sem("w_lo_done")
        pool_init = sem("pool_init")
        pool_zero = sem("pool_zero")
        stack_init = sem("stack_init")
        job_done = sem("job_done")
        sc_max = sem("sc_max")
        sc_exp = sem("sc_exp")
        av_done = sem("av_done")
        sum_done = sem("sum_done")
        mxT_done = sem("mxT_done")
        max_done = sem("max_done")
        mx_split = sem("mx_split")
        mx_rows = sem("mx_rows")
        exp_done = sem("exp_done")
        psumk_done = sem("psumk_done")
        recip_done = sem("recip_done")
        at_f_done = sem("at_f_done")
        at_hi_done = sem("at_hi_done")
        at_lo_done = sem("at_lo_done")
        q_hi_done, q_lo_done = sem("q_hi_done"), sem("q_lo_done")
        k_f_done, k_hi_done, k_lo_done = sem("k_f_done"), sem("k_hi_done"), sem("k_lo_done")
        q_spill, k_spill = sem("q_spill"), sem("k_spill")
        q_stack, k_stack = sem("q_stack"), sem("k_stack")
        keep_in = sem("keep_in")
        keep_done = sem("keep_done")
        row_done = sem("row_done")
        row_stack = sem("row_stack")
        v_done = sem("v_done")
        x_in = sem("x_in")
        bn1, mv1 = sem("bn1"), sem("mv1")
        rstd1 = sem("rstd1")
        xn1 = sem("xn1")
        xT_hi_done, xT_lo_done = sem("xT_hi_done"), sem("xT_lo_done")
        ctx_in = [sem(f"ctx_in{i}") for i in range(2)]
        ctx_hi_done, ctx_lo_done = sem("ctx_hi_done"), sem("ctx_lo_done")
        xres_in = sem("xres_in")
        xres_b = sem("xres_b")
        x2_done = sem("x2_done")
        x2_out = sem("x2_out")
        bn2, mv2 = sem("bn2"), sem("mv2")
        rstd2 = sem("rstd2")
        stats_seen = sem("stats_seen")
        xn2 = sem("xn2")
        xn2_out = sem("xn2_out")
        xnT_done = sem("xnT_done")
        rscore_done = sem("rscore_done")
        rscore_out = sem("rscore_out")
        rscore_seen = sem("rscore_seen")

        JOBS = [
            [[("v", 1)], [], [], [("v", 2)], [("v", 3)]],
            [[("k", 3)], [], [], [("o", 0)], [("o", 1)]],
            [[("o", 2)], [], [], [("o", 3)], []],
            [[("q", 3)], [], [("lt", 0)], [("k", 0)], [("lt", 1)]],
            [[("lt", 2)], [("lt", 3)], [("rt", 0)], [("q", 0)], [("rs", 0)]],
            [[("k", 1)], [("rt", 1)], [("rs", 1)], [("q", 1)], []],
            [[("rt", 2)], [], [("rs", 2)], [("k", 2)], [("rt", 3)]],
            [[("q", 2)], [("rs", 3)], [], [("v", 0)], []],
        ]
        WEIGHT_ORDER = "kqvo"
        OF_BATCH_BEFORE = ("o", "rt", "rs")
        OF_BATCH_AFTER = [("lt", t) for t in range(KT)] + [(kind, t) for t in range(3) for kind in "kq"] + [("v", 0)]
        PROLOGUE = OF_BATCH_AFTER
        READ_BESIDE = [range(0, 2), range(2, 6), range(6, 8), range(8, len(PROLOGUE))]
        EPILOGUE = [("o", t) for t in range(KT)] + [(k, t) for t in range(KT) for k in ("rt", "rs")]
        PER_BATCH = sum(len(place) for slot in JOBS for place in slot)
        JOBS_END = PER_BATCH * B - len(EPILOGUE)
        assert len(EPILOGUE) % 2 == 0 and PER_BATCH % 2 == 0

        def jobs_of(first, last):
            n, table = 0, []
            for u, places in enumerate(JOBS):
                table.append([])
                for place in places:
                    row = []
                    for kind, t in place:
                        if first and kind in OF_BATCH_BEFORE:
                            continue
                        if last and (kind, t) in OF_BATCH_AFTER:
                            continue
                        row.append((kind, t, n))
                        n += 1
                    table[-1].append(row)
            return table

        def job_base(b):
            return len(PROLOGUE) + PER_BATCH * b - (0 if isinstance(b, int) and b == 0 else len(EPILOGUE))

        def bank_of(n):
            return ps_job[(len(PROLOGUE) + n) % 2]

        def read_out(b, kind, t):
            return {
                "q": lambda: (q_lo_done, group(b, t) + 1),
                "k": lambda: (k_f_done, group(b, t) + 1),
                "v": lambda: (v_done, of_values(b, t)),
                "o": lambda: (x2_done, KT * (b - 1) + t + 1),
                "rt": lambda: (xnT_done, KT * (b - 1) + t + 1),
                "rs": lambda: (rscore_done, KT * (b - 1) + t + 1),
                "lt": lambda: (xT_lo_done, KT * (b + 1) + t + 1),
            }[kind]()

        def jobs_done(b, first, last, kind, t):
            for places in jobs_of(first, last):
                for row in places:
                    for k, a, n in row:
                        if (k, a) == (kind, t):
                            return job_base(b) + n + 1
            raise KeyError(kind)

        def need(eng, s, value):
            if not (isinstance(value, int) and value <= 0):
                eng.wait_ge(s, value)

        def group(b, t):
            return NG * (b + 1) + t if t < 3 else NG * b + t

        def of_values(b, t):
            return KT * (b + 1) + 1 if t == 0 else KT * b + t + 1

        block = ctx.enter_context(nc.Block())

        @block.sync
        def _(sp):
            def by_head(dram, part):
                return dram[:, part, :].rearrange("(h r) s -> r h s", r=DK)

            def rows(dram, b, t):
                return dram[bass.ds(b, 1), t * P:(t + 1) * P, :].rearrange("o p d -> p (o d)")

            def load_x(b):
                sp.dma_start(tok[:, :, :], x[bass.ds(b, 1)].rearrange("o (t p) d -> p (o t) d", p=P)).then_inc(x_in, 16)

            def load_keep(b):
                sp.dma_start(keep[:, :].bitcast(I32), mask[bass.ds(b, 1), :].broadcast_to([P, S])).then_inc(keep_in, 16)

            def load_ctx(b, t):
                sp.dma_start(ctx_f[:, t % 2, :], rows(ctxT, b, t)).then_inc(ctx_in[t % 2], 16)

            def load_residual(b):
                sp.dma_start(tok2[:, :, :], x[bass.ds(b, 1)].rearrange("o (t p) d -> p (o t) d", p=P)).then_inc(xres_in, 16)

            def spill_q(g, t):
                sp.wait_ge(q_hi_done, g + 1)
                sp.wait_ge(q_lo_done, g + 1)
                sp.dma_start(q_parts[t], q_st[:, :, :].bitcast(F32)).then_inc(q_spill, 16)

            def spill_k(g, t):
                sp.wait_ge(k_hi_done, g + 1)
                sp.wait_ge(k_lo_done, g + 1)
                sp.dma_start(k_parts[t], k_st[:, :, :].bitcast(F32)).then_inc(k_spill, 16)

            def stack(g, t):
                sp.wait_ge(q_spill, 16 * (g + 1))
                need(sp, sc_exp, 2 * KT * (2 * g - 2))
                for row, part in enumerate((0, 1, 0)):
                    sp.dma_start(qs[row * DK:(row + 1) * DK, t % 2, :, :].bitcast(F32), by_head(q_parts[t], part)).then_inc(q_stack, 16)
                sp.wait_ge(k_spill, 16 * (g + 1))
                for row, part in enumerate((0, 0, 1)):
                    sp.dma_start(ks[row * DK:(row + 1) * DK, t % 2, :, :].bitcast(F32), by_head(k_parts[t], part)).then_inc(k_stack, 16)

            def stack_row(b, par):
                sp.wait_ge(row_done, 2 * b + par + 1)
                for h in range(1, HG):
                    sp.dma_start(ks[ROWS_MASK:ROWS_MAX, par, h, :].bitcast(F32), ks[ROWS_MASK:ROWS_MAX, par, 0, :].bitcast(F32)).then_inc(row_stack, 16)

            def stack_max(unit, u):
                par, q0 = (u // 2) % 2, (u % 2) * QW
                sp.wait_ge(mx_split, 2 * unit + 2)
                for row, src in ((0, mx_hi), (1, mx_lo)):
                    sp.dma_start(qs[ROWS_MAX + row:ROWS_MAX + row + 1, par, :, q0:q0 + QW].bitcast(F32),
                                 src.bitcast(F32)).then_inc(mx_rows, 16)

            def store_x2(b, t):
                sp.wait_ge(x2_done, KT * b + t + 1)
                sp.dma_start(rows(out, b, t), tok2[:, t, :]).then_inc(x2_out, 16)

            def store_xn(b):
                sp.wait_ge(xn2, KT * (b + 1))
                sp.dma_start(xn_dram[bass.ds(b, 1)].rearrange("o (t p) d -> p (o t) d", p=P), tok2[:, :, :]).then_inc(xn2_out, 16)

            def store_router(b, t):
                sp.wait_ge(rscore_done, KT * b + t + 1)
                sp.dma_start(router_dram[bass.ds(b, 1), :, t * P:(t + 1) * P].rearrange("o e p -> e (o p)"), rscore[:, :]).then_inc(rscore_out, 16)

            load_x(0)
            load_ctx(0, 0)
            load_ctx(0, 1)
            for dst, src in ((b_q, bq), (b_k, bk), (b_v, bv)):
                sp.dma_start(dst[:, :], src).then_inc(consts_in, 16)
            sp.dma_start(bo_row[:, :], bo.rearrange("(o d) -> o d", o=1).broadcast_to([P, D])).then_inc(consts_in, 16)
            sp.dma_start(wg[:, :, :], wgT).then_inc(consts_in, 16)
            load_keep(0)
            for n, name in enumerate(WEIGHT_ORDER):
                if n >= 2:
                    sp.wait_ge(w_lo_done, n - 1)
                sp.dma_start(w_f[:, n % 2], wT[name].rearrange("(c p) d -> p c d", p=P)).then_inc(w_in[n % 2], 16)
                if n == 1:
                    for t in range(2, CT):
                        sp.wait_ge(ctx_lo_done, t - 1)
                        load_ctx(0, t)
            stack_row(0, 0)
            spill_k(0, 0)
            spill_q(0, 0)
            stack(0, 0)
            for t in (1, 2):
                spill_k(t, t)
                spill_q(t, t)
            stack_max(0, 0)

            def body(b, first, last):
                table = jobs_of(first, last)
                for u in range(UNITS):
                    unit, next_u = UNITS * b + u, (u + 1) % UNITS
                    made = [(kind, t, place) for place in range(5) for kind, t, _ in table[u][place]]
                    if u == 0 and not last:
                        sp.wait_ge(xT_lo_done, KT * (b + 1))
                        load_x(b + 1)
                    if u >= 5 and not first:
                        store_router(b - 1, u - 5)
                    if u % 2 == 0 and not (last and u == 6):
                        t = (u // 2 + 1) % NG
                        stack(NG * b + u // 2 + 1, t)
                    if u == 0:
                        stack_row(b, 1)
                    if u == 6 and not last:
                        stack_row(b + 1, 0)
                    if u == 7:
                        if not first:
                            sp.wait_ge(xn2_out, 16 * b)
                            sp.wait_ge(xnT_done, KT * b)
                        load_residual(b)
                    if u == 1 and not last:
                        load_ctx(b + 1, 0)
                        load_ctx(b + 1, 1)
                    if u == 2 and not last:
                        for t in range(2, CT):
                            sp.wait_ge(ctx_lo_done, CT * (b + 1) + t - 1)
                            load_ctx(b + 1, t)
                    for kind, t, place in made:
                        if kind == "q" and place == 0:
                            spill_q(group(b, t), t)
                    if not (last and u == UNITS - 1):
                        stack_max(unit + 1, next_u)
                    for kind, t, place in made:
                        if kind == "k":
                            spill_k(group(b, t), t)
                        elif kind == "q" and place > 0:
                            spill_q(group(b, t), t)
                    if u == 1 and not last:
                        sp.wait_ge(k_f_done, NG * (b + 1))
                        load_keep(b + 1)
                    if u == 1 and not first:
                        store_x2(b - 1, 0)
                        store_x2(b - 1, 1)
                    if u == 2 and not first:
                        store_x2(b - 1, 2)
                        store_x2(b - 1, 3)
                    if u == 4 and not first:
                        store_xn(b - 1)
                    if u == 7 and not first:
                        store_router(b - 1, 3)
                        sp.wait_ge(rscore_out, 16 * KT * b)
                        sp.sem_inc(rscore_seen, 1)

            over_batches(sp, B, body)
            for t in range(KT):
                store_x2(B - 1, t)
            store_xn(B - 1)
            for t in range(KT):
                store_router(B - 1, t)
            sp.wait_ge(x2_out, 16 * KT * B)
            sp.wait_ge(xn2_out, 16 * B)
            sp.wait_ge(rscore_out, 16 * KT * B)

        @block.tensor
        def _(pe):
            def product3(dst, a_hi, a_lo, b_hi, b_lo):
                for c in range(CT):
                    for i, (l, r) in enumerate(((a_hi, b_hi), (a_hi, b_lo), (a_lo, b_hi))):
                        last = nc.tensor.matmul(dst, l(c), r(c), start=(c == 0 and i == 0), stop=(c == CT - 1 and i == 2))
                return last

            def job(b, kind, t, bank, before):
                if before is not None:
                    pe.wait_ge(*before)
                if kind in "qk":
                    g = slice(t * P, (t + 1) * P)
                    if kind == "q":
                        src_hi, src_lo = xT_hi, xT_lo
                    else:
                        src_hi, src_lo = ctx_hi, ctx_lo
                    if t < 3:
                        nb = b + 1
                        if kind == "q":
                            pe.wait_ge(xT_lo_done, KT * (nb + 1))
                        else:
                            pe.wait_ge(ctx_lo_done, CT * (nb + 1))
                    wh, wl = w_hi[kind], w_lo[kind]
                    last = product3(bank[:, :], lambda c: wh[:, c, g], lambda c: wl[:, c, g],
                                    lambda c: src_hi[:, c, :], lambda c: src_lo[:, c, :])
                elif kind == "v":
                    s = slice(t * P, (t + 1) * P)
                    last = product3(bank[:, :], lambda c: ctx_hi[:, c, s], lambda c: ctx_lo[:, c, s],
                                    lambda c: w_hi["v"][:, c, :], lambda c: w_lo["v"][:, c, :])
                elif kind == "o":
                    s = slice(t * P, (t + 1) * P)
                    if t == 0:
                        pe.wait_ge(at_lo_done, UNITS * b)
                    last = product3(bank[:, :], lambda c: at_hi[:, c, s], lambda c: at_lo[:, c, s],
                                    lambda c: w_hi["o"][:, c, :], lambda c: w_lo["o"][:, c, :])
                elif kind in ("lt", "rt"):
                    if kind == "lt":
                        src = tok
                        pe.wait_ge(xn1, KT * (b + 1) + t + 1)
                    else:
                        src = tok2
                        pe.wait_ge(xn2, KT * (b - 1) + t + 1)
                    for c in range(CT):
                        last = nc.tensor.matmul(bank[:, c * P:(c + 1) * P], src[:, t, c * P:(c + 1) * P], ident[:, :],
                                                is_transpose=True, start=True, stop=True)
                elif kind == "rs":
                    pe.wait_ge(xnT_done, KT * (b - 1) + t + 1)
                    for c in range(CT):
                        last = nc.tensor.matmul(bank[0:E, 0:P], wg[:, c, :], xnT[:, c * P:(c + 1) * P],
                                                start=(c == 0), stop=(c == CT - 1))
                last.then_inc(job_done, 1)

            def scores_max(unit, u, pair):
                par, q0 = (u // 2) % 2, (u % 2) * QW
                if pair == 0:
                    need(pe, mx_split, 2 * unit)
                else:
                    pe.wait_ge(max_done, HG * unit + pair)
                for qt in range(QT):
                    q = slice(q0 + qt * P, q0 + (qt + 1) * P)
                    last = nc.tensor.matmul(ps_max[:, qt, :], qs[0:ROWS_MAX, par, pair, q], ks[0:ROWS_MAX, par, pair, :],
                                            start=True, stop=True)
                last.then_inc(sc_max, 1)

            def scores_exp(unit, u, kt):
                par, q0 = (u // 2) % 2, (u % 2) * QW
                if kt == 0:
                    pe.wait_ge(mx_rows, MX_ROWS * (unit + 1))
                for pair in range(2):
                    need(pe, exp_done, 2 * (KT * unit + kt) - 1 + pair)
                    for h in (2 * pair, 2 * pair + 1):
                        last = nc.tensor.matmul(ps_exp[:, h, :], ks[0:ROWS, par, h, kt * P:(kt + 1) * P],
                                                qs[0:ROWS, par, h, q0:q0 + QW], start=True, stop=True)
                    last.then_inc(sc_exp, 1)

            def maxima(unit):
                pe.wait_ge(max_done, HG * unit + HG)
                for qt in range(QT):
                    last = nc.tensor.matmul(ps_max[0:HG, 0, qt * P:(qt + 1) * P], mx[:, qt, :], ident[:, :],
                                            is_transpose=True, start=True, stop=True)
                last.then_inc(mxT_done, 1)

            def probs_v(unit, u, b, kt, av_bank):
                g = u // 2
                pe.wait_ge(exp_done, 2 * (KT * unit + kt + 1))
                if kt == 0:
                    need(pe, at_f_done, unit - 1)
                if u == 0:
                    pe.wait_ge(v_done, KT * b + kt + 1)
                for h in range(HG):
                    last = nc.tensor.matmul(ps_av[av_bank][h * DK:(h + 1) * DK, 0, :],
                                            v[:, kt, (g * HG + h) * DK:(g * HG + h + 1) * DK], probs[:, kt, h, :],
                                            start=(kt == 0), stop=(kt == KT - 1), tile_position=(0, h * DK))
                last.then_inc(av_done, 1)

            def sums(unit, av_bank):
                pe.wait_ge(psumk_done, 3 * unit + 3)
                for h in range(HG):
                    last = nc.tensor.matmul(ps_av[av_bank][h * DK:(h + 1) * DK, 1, :], ones[:, :], psumk[:, h, :],
                                            start=True, stop=True, tile_position=(0, h * DK))
                last.then_inc(sum_done, 1)

            pe.wait_ge(consts_in, 5 * 16)
            pe.wait_ge(pool_init, POOL_INIT)
            for n, (kind, t) in enumerate(PROLOGUE):
                if t == 0 and kind in WEIGHT_ORDER:
                    pe.wait_ge(w_lo_done, 4 if kind == "v" else WEIGHT_ORDER.index(kind) + 1)
                job(-1, kind, t, ps_job[n % 2], read_out(-1, *PROLOGUE[n - 2]) if n >= 2 else None)
            pe.wait_ge(q_stack, 3 * 16)
            pe.wait_ge(k_stack, 3 * 16)
            pe.wait_ge(row_stack, 3 * 16)
            for pair in range(HG):
                scores_max(0, 0, pair)
            maxima(0)

            def body(b, first, last):
                table = jobs_of(first, last)
                order = [(kind, t) for places in table for row in places for kind, t, _ in row]
                for u in range(UNITS):
                    unit = UNITS * b + u
                    has_next = not (last and u == UNITS - 1)
                    nu = (u + 1) % UNITS
                    has_prev = not (first and u == 0)
                    bank, prev_bank = u % 2, (u + 1) % 2

                    def fill(place):
                        for kind, t, n in table[u][place]:
                            before = read_out(b, *order[n - 2]) if n >= 2 else read_out(b - 1, *PROLOGUE[n - 2])
                            job(b, kind, t, bank_of(n), before)

                    if has_next:
                        if u % 2 == 1:
                            g = NG * b + u // 2 + 1
                            pe.wait_ge(q_stack, 48 * g + 48)
                            pe.wait_ge(k_stack, 48 * g + 48)
                            if u == 1:
                                pe.wait_ge(row_stack, 96 * b + 96)
                            if u == UNITS - 1:
                                pe.wait_ge(row_stack, 96 * b + 96 + 48)
                        scores_max(unit + 1, nu, 0)
                    if has_prev:
                        probs_v(unit - 1, (u - 1) % UNITS, b - 1 if u == 0 else b, 2, prev_bank)
                    fill(0)
                    scores_exp(unit, u, 0)
                    if has_next:
                        scores_max(unit + 1, nu, 1)
                    if has_prev:
                        probs_v(unit - 1, (u - 1) % UNITS, b - 1 if u == 0 else b, 3, prev_bank)
                    fill(1)
                    scores_exp(unit, u, 1)
                    if has_next:
                        scores_max(unit + 1, nu, 2)
                    if has_prev:
                        sums(unit - 1, prev_bank)
                    probs_v(unit, u, b, 0, bank)
                    scores_exp(unit, u, 2)
                    if has_next:
                        scores_max(unit + 1, nu, 3)
                    probs_v(unit, u, b, 1, bank)
                    fill(2)
                    scores_exp(unit, u, 3)
                    if has_next:
                        maxima(unit + 1)
                    fill(3)
                    fill(4)

            over_batches(pe, B, body)
            end = UNITS * B - 1
            probs_v(end, UNITS - 1, B - 1, 2, end % 2)
            probs_v(end, UNITS - 1, B - 1, 3, end % 2)
            sums(end, end % 2)
            last_jobs = [(kind, t) for places in jobs_of(False, True) for row in places for kind, t, _ in row]
            for n, (kind, t) in enumerate(EPILOGUE):
                before = read_out(B, *EPILOGUE[n - 2]) if n >= 2 else read_out(B - 1, *last_jobs[n - 2])
                job(B, kind, t, ps_job[(JOBS_END + n) % 2], before)

        @block.scalar
        def _(act):
            def read(b, kind, t, bank, done):
                g = group(b, t) if kind in ("q", "k") else None
                if kind == "q":
                    act.wait_ge(job_done, done)
                    need(act, q_spill, 16 * g)
                    nc.scalar.activation(q_st[:, 0, :], bank[:, :], ACT.Identity, bias=b_q[:, t:t + 1]).then_inc(q_hi_done, 1)
                elif kind == "k":
                    act.wait_ge(k_f_done, g + 1)
                    nc.scalar.activation(k_st[:, 0, :], k_st[:, 1, :].bitcast(F32), ACT.Copy).then_inc(k_hi_done, 1)
                elif kind == "v":
                    act.wait_ge(job_done, done)
                    need(act, av_done, KT * (UNITS * (b + (1 if t == 0 else 0)) - 1) + t + 1)
                    nc.scalar.activation(v[:, t, :], bank[:, :], ACT.Copy).then_inc(v_done, 1)
                elif kind == "lt":
                    act.wait_ge(job_done, done)
                    nc.scalar.activation(xT_hi[:, :, t * P:(t + 1) * P], bank[:, :].rearrange("p (c q) -> p c q", c=CT), ACT.Copy).then_inc(xT_hi_done, 1)
                elif kind == "rt":
                    act.wait_ge(job_done, done)
                    if t == 0 and not (isinstance(b, int) and b >= B - 1):
                        act.wait_ge(ctx_lo_done, CT * (b + 2))
                    nc.scalar.activation(xnT, bank[:, :], ACT.Copy).then_inc(xnT_done, 1)

            def split_ctx(b, t, uses):
                act.wait_ge(ctx_in[t % 2], 16 * (2 * b + t // 2 + 1))
                if uses is not None:
                    act.wait_ge(job_done, uses)
                nc.scalar.activation(ctx_hi[:, t, :], ctx_f[:, t % 2, :], ACT.Copy).then_inc(ctx_hi_done, 1)

            def split_w(n, name):
                act.wait_ge(w_in[n % 2], 16 * (n // 2 + 1))
                nc.scalar.activation(w_hi[name][:, :, :], w_f[:, n % 2], ACT.Copy).then_inc(w_hi_done, 1)

            def exponentials(unit, kt):
                need(act, av_done, KT * (unit - 1) + kt + 1)
                need(act, psumk_done, 3 * (unit - 1) + max(1, kt))
                for pair in range(2):
                    h = slice(2 * pair, 2 * pair + 2)
                    act.wait_ge(sc_exp, 2 * (KT * unit + kt) + pair + 1)
                    nc.scalar.activation(probs[:, kt, h, :], ps_exp[:, h, :], ACT.Exp, scale=SCALE).then_inc(exp_done, 1)

            def output_hi(unit, u, o_done):
                g, q = u // 2, slice((u % 2) * QW, (u % 2 + 1) * QW)
                act.wait_ge(at_f_done, unit + 1)
                if o_done is not None:
                    act.wait_ge(job_done, o_done)
                nc.scalar.activation(at_hi[:, g, q], at_f[:, :], ACT.Identity, bias=b_v[:, g:g + 1]).then_inc(at_hi_done, 1)

            act.wait_ge(consts_in, 5 * 16)
            split_ctx(0, 0, None)
            split_ctx(0, 1, None)
            for n, name in enumerate(WEIGHT_ORDER):
                split_w(n, name)
                if n == 1:
                    split_ctx(0, 2, None)
                    split_ctx(0, 3, None)
                for i in READ_BESIDE[n]:
                    read(-1, *PROLOGUE[i], ps_job[i % 2], i + 1)

            def body(b, first, last):
                table = jobs_of(first, last)
                for u in range(UNITS):
                    unit = UNITS * b + u

                    def fill(place):
                        for kind, t, n in table[u][place]:
                            read(b, kind, t, bank_of(n), job_base(b) + n + 1)

                    fill(0)
                    exponentials(unit, 0)
                    fill(1)
                    exponentials(unit, 1)
                    if not (first and u < 2):
                        writes = None
                        if not first and u in (2, 3):
                            writes = jobs_done(b, first, last, "o", 1 if u == 2 else 3)
                        output_hi(unit - 2, (u - 2) % UNITS, writes)
                    exponentials(unit, 2)
                    fill(2)
                    exponentials(unit, 3)
                    fill(3)
                    fill(4)
                    if u in (1, 2) and not last:
                        for t in range(2):
                            split_ctx(b + 1, 2 * (u - 1) + t, jobs_done(b, first, last, "k", 3))
            over_batches(act, B, body)
            output_hi(UNITS * B - 2, UNITS - 2, None)
            output_hi(UNITS * B - 1, UNITS - 1, None)
            for n, (kind, t) in enumerate(EPILOGUE):
                read(B, kind, t, ps_job[(JOBS_END + n) % 2], JOBS_END + n + 1)

        @block.vector
        def _(dve):
            def read(b, kind, t, bank, done):
                if kind == "q":
                    g = group(b, t)
                    dve.wait_ge(q_hi_done, g + 1)
                    need(dve, q_spill, 16 * g)
                    nc.vector.scalar_tensor_tensor(out=q_st[:, 1, :], in0=bank[:, :], scalar=b_q[:, t:t + 1], in1=q_st[:, 0, :].bitcast(F32),
                                                   op0=ALU.add, op1=ALU.subtract).then_inc(q_lo_done, 1)
                elif kind == "k":
                    g = group(b, t)
                    dve.wait_ge(job_done, done)
                    need(dve, k_spill, 16 * g)
                    nc.vector.scalar_tensor_tensor(out=k_st[:, 1, :].bitcast(F32), in0=bank[:, :], scalar=b_k[:, t:t + 1], in1=keep[:, :],
                                                   op0=ALU.add, op1=ALU.mult).then_inc(k_f_done, 1)
                elif kind == "o":
                    dve.wait_ge(job_done, done)
                    dve.wait_ge(xres_b, KT * (b - 1) + t + 1)
                    nc.vector.tensor_tensor(out=tok2[:, t, :], in0=bank[:, :], in1=tok2[:, t, :], op=ALU.add).then_inc(x2_done, 1)
                    dve.wait_ge(x2_done, KT * (b - 1) + t + 1)
                    nc.vector.bn_stats(out=stats[:, 1, t, :], in_=tok2[:, t, :]).then_inc(bn2, 1)
                    if t == KT - 1:
                        dve.wait_ge(bn2, KT * b)
                        dve.sem_inc(stats_seen, 1)
                        for i in range(KT):
                            nc.vector.bn_aggr(out=mv[:, 1, i, :], in_=stats[:, 1, i, :]).then_inc(mv2, 1)
                elif kind == "rs":
                    dve.wait_ge(job_done, done)
                    if t > 0:
                        dve.wait_ge(rscore_out, 16 * (KT * (b - 1) + t))
                    nc.vector.tensor_copy(rscore[:, :], bank[0:E, 0:P]).then_inc(rscore_done, 1)
                elif kind == "lt":
                    dve.wait_ge(xT_hi_done, KT * (b + 1) + t + 1)
                    s = slice(t * P, (t + 1) * P)
                    nc.vector.tensor_tensor(out=xT_lo[:, :, s], in0=bank[:, :].rearrange("p (c q) -> p c q", c=CT),
                                            in1=xT_hi[:, :, s].bitcast(F32), op=ALU.subtract).then_inc(xT_lo_done, 1)

            def keep_from_mask(b):
                dve.wait_ge(keep_in, 16 * (b + 1))
                nc.vector.tensor_scalar(out=keep[:, :], in0=keep[:, :].bitcast(I32), scalar1=0, scalar2=None,
                                        op0=ALU.not_equal).then_inc(keep_done, 1)

            def mask_row(b, par):
                dve.wait_ge(keep_done, b + 1)
                need(dve, sc_exp, 2 * KT * (UNITS * (b - 1) + 6 + 2 * par))
                nc.vector.tensor_scalar(out=ks[ROWS_MASK:ROWS_MAX, par, 0, :], in0=keep[ROWS_MASK:ROWS_MAX, :], scalar1=0.0,
                                        scalar2=masked[ROWS_MASK:ROWS_MAX, :], op0=ALU.is_equal, op1=ALU.mult).then_inc(row_done, 1)

            def maximum(unit, pair):
                dve.wait_ge(sc_max, HG * unit + pair + 1)
                nc.vector.tensor_reduce(out=mx[:, :, pair], in_=ps_max[:, :, :], axis=AX_X, op=ALU.max).then_inc(max_done, 1)

            def split_maxima(unit):
                dve.wait_ge(mxT_done, unit + 1)
                need(dve, mx_rows, MX_ROWS * unit)
                nc.vector.tensor_copy(mx_hi, ps_max[0:HG, 0, 0:QW]).then_inc(mx_split, 1)
                dve.wait_ge(mx_split, 2 * unit + 1)
                nc.vector.tensor_tensor(out=mx_lo, in0=ps_max[0:HG, 0, 0:QW], in1=mx_hi.bitcast(F32),
                                        op=ALU.subtract).then_inc(mx_split, 1)

            def normalise(unit, av_bank):
                dve.wait_ge(sum_done, unit + 1)
                need(dve, at_lo_done, unit)
                nc.vector.reciprocal(at_f[:, :], ps_av[av_bank][:, 1, :]).then_inc(recip_done, 1)
                dve.wait_ge(recip_done, unit + 1)
                nc.vector.tensor_tensor(out=at_f[:, :], in0=ps_av[av_bank][:, 0, :], in1=at_f[:, :], op=ALU.mult).then_inc(at_f_done, 1)

            def output_lo(unit, u):
                g, q = u // 2, slice((u % 2) * QW, (u % 2 + 1) * QW)
                dve.wait_ge(at_hi_done, unit + 1)
                nc.vector.scalar_tensor_tensor(out=at_lo[:, g, q], in0=at_f[:, :], scalar=b_v[:, g:g + 1], in1=at_hi[:, g, q].bitcast(F32),
                                               op0=ALU.add, op1=ALU.subtract).then_inc(at_lo_done, 1)

            def statistics(b, tiles=range(KT)):
                dve.wait_ge(x_in, 16 * (b + 1))
                for t in tiles:
                    nc.vector.bn_stats(out=stats[:, 0, t, :], in_=tok[:, t, :]).then_inc(bn1, 1)
                dve.wait_ge(bn1, KT * b + tiles[-1] + 1)
                dve.sem_inc(stats_seen, 1)
                for t in tiles:
                    nc.vector.bn_aggr(out=mv[:, 0, t, :], in_=stats[:, 0, t, :]).then_inc(mv1, 1)

            def apply_norm(tokens, which, done, tiles=range(KT)):
                for t in tiles:
                    nc.vector.tensor_scalar(out=tokens[:, t, :], in0=tokens[:, t, :], scalar1=mv[:, which, t, 0:1], scalar2=rstd[:, which, t:t + 1],
                                            op0=ALU.subtract, op1=ALU.mult).then_inc(done, 1)

            nc.vector.memset(qs[ROWS_MASK:P, :, :, :].bitcast(F32), 1.0).then_inc(stack_init, 1)
            dve.wait_ge(consts_in, 5 * 16)
            dve.wait_ge(pool_init, POOL_INIT)
            statistics(0)
            dve.wait_ge(rstd1, 2)
            apply_norm(tok, 0, xn1)
            dve.wait_ge(stack_init, 2)
            keep_from_mask(0)
            mask_row(0, 0)
            for n, name in enumerate(WEIGHT_ORDER):
                dve.wait_ge(w_hi_done, n + 1)
                nc.vector.tensor_tensor(out=w_lo[name][:, :, :], in0=w_f[:, n % 2], in1=w_hi[name][:, :, :].bitcast(F32),
                                        op=ALU.subtract).then_inc(w_lo_done, 1)
                for i in READ_BESIDE[n]:
                    read(-1, *PROLOGUE[i], ps_job[i % 2], i + 1)
            for pair in range(HG):
                maximum(0, pair)
            split_maxima(0)
            maximum(1, 0)

            def body(b, first, last):
                table = jobs_of(first, last)
                for u in range(UNITS):
                    unit = UNITS * b + u
                    has_next = not (last and u == UNITS - 1)
                    has_prev = not (first and u == 0)

                    def fill(place):
                        for kind, t, n in table[u][place]:
                            read(b, kind, t, bank_of(n), job_base(b) + n + 1)

                    def late():
                        if u in (0, 1) and not last:
                            statistics(b + 1, (2 * u, 2 * u + 1))
                        if u == 2 and not last:
                            keep_from_mask(b + 1)
                            dve.wait_ge(rstd1, 2 * (b + 2))
                            apply_norm(tok, 0, xn1, (0, 1))
                        if u == 3 and not last:
                            apply_norm(tok, 0, xn1, (2, 3))
                        if u == 4 and not first:
                            apply_norm(tok2, 1, xn2, (2, 3))

                    if u == 0:
                        mask_row(b, 1)
                    if u == 6 and not last:
                        mask_row(b + 1, 0)
                    fill(0)
                    if u == 4 and not first:
                        dve.wait_ge(x2_out, 16 * KT * b)
                        dve.wait_ge(rstd2, 2 * b)
                        apply_norm(tok2, 1, xn2, (0, 1))
                    if has_next:
                        maximum(unit + 1, 1)
                    fill(1)
                    if has_next:
                        maximum(unit + 1, 2)
                    if not (first and u < 2):
                        output_lo(unit - 2, (u - 2) % UNITS)
                    if has_next:
                        maximum(unit + 1, 3)
                    fill(2)
                    if has_next:
                        split_maxima(unit + 1)
                    if has_prev:
                        normalise(unit - 1, (u + 1) % 2)
                    fill(3)
                    late()
                    if has_next and not (last and u == UNITS - 2):
                        maximum(unit + 2, 0)
                    fill(4)

            over_batches(dve, B, body)
            end = UNITS * B - 1
            output_lo(end - 1, UNITS - 2)
            normalise(end, end % 2)
            output_lo(end, UNITS - 1)
            for n, (kind, t) in enumerate(EPILOGUE):
                read(B, kind, t, ps_job[(JOBS_END + n) % 2], JOBS_END + n + 1)
                if (kind, t) == ("o", KT - 1):
                    dve.wait_ge(x2_out, 16 * KT * B)
                    dve.wait_ge(rstd2, 2 * B)
                    apply_norm(tok2, 1, xn2)

        @block.gpsimd
        def _(pool):
            def inverse_sigma(which, stats_done, count, done, made):
                pool.wait_ge(stats_done, count)
                nc.gpsimd.tensor_tensor(out=rstd[:, which, :], in0=mv[:, which, :, 1], in1=eps[:, :], op=ALU.add).then_inc(done, 1)
                pool.wait_ge(done, made + 1)
                nc.gpsimd.tensor_tensor(out=rstd[:, which, :], in0=rstd[:, which, :], in1=half[:, :], op=ALU.pow).then_inc(done, 1)

            def ctx_rest(b, t):
                pool.wait_ge(ctx_hi_done, CT * b + t + 1)
                nc.gpsimd.tensor_tensor(out=ctx_lo[:, t, :], in0=ctx_f[:, t % 2, :], in1=ctx_hi[:, t, :].bitcast(F32),
                                        op=ALU.subtract).then_inc(ctx_lo_done, 1)

            def k_rest(g):
                pool.wait_ge(k_hi_done, g + 1)
                nc.gpsimd.tensor_tensor(out=k_st[:, 1, :], in0=k_st[:, 1, :].bitcast(F32), in1=k_st[:, 0, :].bitcast(F32), op=ALU.subtract).then_inc(k_lo_done, 1)

            def residual_bias(b, t):
                pool.wait_ge(xres_in, 16 * (b + 1))
                nc.gpsimd.tensor_tensor(out=tok2[:, t, :], in0=tok2[:, t, :], in1=bo_row[:, :], op=ALU.add).then_inc(xres_b, 1)

            def add_up(unit, step):
                pool.wait_ge(exp_done, 2 * (KT * unit + step + 2))
                if step == 0:
                    need(pool, sum_done, unit)
                else:
                    pool.wait_ge(psumk_done, 3 * unit + step)
                nc.gpsimd.tensor_tensor(out=psumk[:, :, :], in0=probs[:, 0] if step == 0 else psumk[:, :, :], in1=probs[:, step + 1],
                                        op=ALU.add).then_inc(psumk_done, 1)

            nc.gpsimd.memset(ident[:, :], 0.0).then_inc(pool_zero, 1)
            nc.gpsimd.memset(masked[:, :], MASK_HI).then_inc(pool_zero, 1)
            nc.gpsimd.memset(half[:, :], -0.5).then_inc(pool_init, 1)
            nc.gpsimd.memset(eps[:, :], EPS).then_inc(pool_init, 1)
            nc.gpsimd.memset(ones[:, :], 1.0).then_inc(pool_init, 1)
            pool.wait_ge(pool_zero, 2)
            nc.gpsimd.affine_select(out=ident[:, :], in_=ident[:, :], compare_op=ALU.not_equal, fill=1.0, base=0,
                                    pattern=[[-1, P]], channel_multiplier=1).then_inc(pool_init, 1)
            nc.gpsimd.affine_select(out=masked[:, :], in_=masked[:, :], compare_op=ALU.not_equal, fill=MASK_LO, base=-(ROWS_MASK + 1),
                                    pattern=[[0, 1]], channel_multiplier=1).then_inc(pool_init, 1)
            pool.wait_ge(pool_init, POOL_INIT)
            nc.gpsimd.memset(ks[ROWS_MASK:P, :, :, :].bitcast(F32), -1.0).then_inc(stack_init, 1)
            pool.wait_ge(stack_init, 2)
            ctx_rest(0, 0)
            ctx_rest(0, 1)
            inverse_sigma(0, mv1, KT, rstd1, 0)
            ctx_rest(0, 2)
            ctx_rest(0, 3)
            pool.wait_ge(consts_in, 5 * 16)
            for g in range(3):
                k_rest(g)

            def body(b, first, last):
                table = jobs_of(first, last)
                for u in range(UNITS):
                    unit = UNITS * b + u

                    def keys(*places):
                        for place in places:
                            for kind, t, _ in table[u][place]:
                                if kind == "k":
                                    k_rest(group(b, t))

                    def next_ctx(slot, t):
                        if u == slot and not last:
                            ctx_rest(b + 1, t)

                    def residual(slot, t):
                        if u == slot and not first:
                            residual_bias(b - 1, t)

                    residual(1, 0)
                    residual(1, 1)
                    next_ctx(2, 0)
                    next_ctx(2, 1)
                    residual(2, 2)
                    residual(2, 3)
                    next_ctx(3, 2)
                    next_ctx(3, 3)
                    if u == 3 and not first:
                        inverse_sigma(1, mv2, KT * b, rstd2, 2 * (b - 1))
                    add_up(unit, 0)
                    keys(0, 1)
                    if u == 2 and not last:
                        inverse_sigma(0, mv1, KT * (b + 2), rstd1, 2 * (b + 1))
                    add_up(unit, 1)
                    keys(2)
                    add_up(unit, 2)
                    keys(3, 4)

            over_batches(pool, B, body)
            for t in range(KT):
                residual_bias(B - 1, t)
            inverse_sigma(1, mv2, KT * B, rstd2, 2 * (B - 1))


def route_constants(batches, experts, tiles):
    row = np.arange(P)
    same = (row[:, None] % experts == row[None, :] % experts).astype(np.float32)
    before = same * (row[:, None] < row[None, :])
    numbers = np.broadcast_to(row[None, :], (P, P))
    tile_ids = np.broadcast_to(np.arange(batches * tiles)[None, :], (P, batches * tiles))
    return np.concatenate([same, before, np.eye(P), numbers, tile_ids, row[:, None]], axis=1).astype(np.float32)


def experts(nc, xn_dram, router_dram, weights, consts, out):
    T, D = xn_dram.shape
    ROWS, S = router_dram.shape
    E, CHUNKS, _, _ = weights.shape
    CAP = T // E
    TILES = T // P
    TB = S // P
    B = ROWS // E
    CT = D // P
    H = 1024
    HALF = CAP // 2
    HT = H // P
    CAPT = CAP // P
    HTT = CAPT // 2
    PARTS = 5
    GROUP = TILES // 4
    DIGITS = 15

    with ExitStack() as ctx:
        def sb(name, shape, dt=F32):
            return ctx.enter_context(nc.sbuf_tensor(name, shape, dt))

        def sem(name):
            return ctx.enter_context(nc.semaphore(name))

        tables = sb("tables", [P, 4 * P + TILES + 1])
        same, before, ident, numbers = (tables[:, i * P:(i + 1) * P] for i in range(4))
        tile_ids = tables[:, 4 * P:4 * P + TILES]
        row_id = tables[:, 4 * P + TILES:4 * P + TILES + 1]
        numbers_b = sb("numbers_b", [P, P], BF16)
        loT = sb("loT", [P, B, TB, E], BF16)
        hiT = sb("hiT", [P, B, TB, E], BF16)
        wT = [sb(f"wT{i}", [P, B, TB, E], BF16) for i in range(3)]
        w_stage = sb("w_stage", [P, 2, 4 * 512])
        w_hi = [sb(f"ew{k}_hi", [P, 4, 512], F32R) for k in range(CHUNKS)]
        w_lo = [sb(f"ew{k}_lo", [P, 4, 512], F32R) for k in range(CHUNKS)]
        w_in = [sem(f"ew_in{i}") for i in range(2)]
        w_hi_done, w_lo_done = sem("ew_hi_done"), sem("ew_lo_done")

        def load_w(sp, e, k):
            if not (isinstance(e, int) and CHUNKS * e + k < 2):
                sp.wait_ge(w_lo_done, CHUNKS * e + k - 1)
            sp.dma_start(w_stage[:, k % 2, :], weights[bass.ds(e, 1), k].rearrange("o p n -> p (o n)")).then_inc(w_in[k % 2], 16)

        with ExitStack() as rctx:
            def rsb(name, shape, dt=F32):
                return rctx.enter_context(nc.sbuf_tensor(name, shape, dt))

            sc = rsb("sc", [P, S])
            work = rsb("work", [P, S])
            ones = rsb("r_ones", [P, S])
            sel = rsb("sel", [P, S])
            eq = rsb("eq", [P, S])
            rank = rsb("rank", [P, S])
            ex = rsb("ex", [P, S])
            place_i = rsb("place_i", [P, S], I32)
            lo_i = rsb("lo_i", [P, S], I32)
            hi_i = rsb("hi_i", [P, S], I32)
            lo = rsb("lo", [P, S])
            hi = rsb("hi", [P, S])
            w = rsb("w", [P, S])
            wrest = rsb("wrest", [P, TB, P])
            thr = rsb("thr", [P, 1], I32)
            digits = rsb("digits", [P, 3], I32)
            digit_one = rsb("digit_one", [P, 1])
            cands = rsb("cands", [P, 3], I32)
            reached = rsb("reached", [P, 3])
            digit = rsb("digit", [P, 1])
            step = rsb("step", [P, 1], I32)
            count = rsb("count", [P, 3])
            stat = rsb("stat", [P, 12])
            top = rsb("top", [P, P])
            top_row = rsb("top_row", [1, 2, P])
            ps_tot = rctx.enter_context(nc.psum_tensor("ps_tot", [P, 512], F32))
            ps_a = rctx.enter_context(nc.psum_tensor("ps_a", [P, 512], F32))
            ps_t = [rctx.enter_context(nc.psum_tensor(f"ps_t{i}", [P, TB, P], F32)) for i in range(3)]

            def rsem(name):
                return rctx.enter_context(nc.semaphore(name))

            r_in = rsem("r_in")
            link_s = rsem("link_s")
            cand_done, count_done = rsem("cand_done"), rsem("count_done")
            total_done, step_done = rsem("total_done"), rsem("step_done")
            thr_done = rsem("thr_done")
            bit_done = rsem("bit_done")
            digit_done = rsem("digit_done")
            asks, answers = rsem("asks"), rsem("answers")
            max_ready, ex_done = rsem("max_ready"), rsem("ex_done")
            lists_ready, listsT = rsem("lists_ready"), rsem("listsT")

            block = rctx.enter_context(nc.Block())

            @block.sync
            def _(sp):
                sp.dma_start(sc[:, :], router_dram).then_inc(r_in, 16)
                sp.dma_start(tables[:, :], consts).then_inc(r_in, 16)
                for k in range(CHUNKS):
                    load_w(sp, 0, k)

            @block.tensor
            def _(pe):
                pe.wait_ge(r_in, 32)
                for i in range(2):
                    pe.wait_ge(count_done, i + 1)
                    nc.tensor.matmul(ps_tot[:, 0:1], same, count[:, 0:1], start=True, stop=True).then_inc(total_done, 1)
                with pe.Fori(1, DIGITS + 1) as i:
                    pe.wait_ge(count_done, 3 * i + 2)
                    nc.tensor.matmul(ps_tot[:, 0:3], same, count[:, :], start=True, stop=True).then_inc(total_done, 1)
                pe.wait_ge(asks, 1)
                nc.tensor.matmul(ps_a[:, 0:1], same, stat[:, 0:1], start=True, stop=True)
                nc.tensor.matmul(ps_a[:, 1:2], before, stat[:, 1:2], start=True, stop=True).then_inc(answers, 1)
                pe.wait_ge(asks, 2)
                nc.tensor.matmul(ps_a[:, 0:1], before, stat[:, 2:3], start=True, stop=True)
                nc.tensor.matmul(ps_a[:, P:2 * P], top[:, :], ident, is_transpose=True, start=True, stop=True).then_inc(answers, 1)
                pe.wait_ge(asks, 3)
                nc.tensor.matmul(ps_a[:, 0:1], top_row[0:1, 1, :], ones[0:1, 0:1], start=True, stop=True).then_inc(answers, 1)
                pe.wait_ge(asks, 4)
                nc.tensor.matmul(ps_a[:, 0:1], same, stat[:, 5:6], start=True, stop=True).then_inc(answers, 1)
                for k, src in enumerate((lo, hi, w)):
                    pe.wait_ge(lists_ready, k + 1)
                    for c in range(TB):
                        last = nc.tensor.matmul(ps_t[k][:, c, :], src[:, c * P:(c + 1) * P], ident, is_transpose=True, start=True, stop=True)
                    last.then_inc(listsT, 1)

            @block.scalar
            def _(act):
                for k in range(CHUNKS):
                    act.wait_ge(w_in[k % 2], 16 * (k // 2 + 1))
                    nc.scalar.activation(w_hi[k][:, :, :], w_stage[:, k % 2, :].rearrange("p (c n) -> p c n", c=4), ACT.Copy).then_inc(w_hi_done, 1)
                act.wait_ge(max_ready, 1)
                nc.scalar.activation(ex[:, :], sc[:, :], ACT.Exp, bias=stat[:, 4:5]).then_inc(ex_done, 1)

            @block.gpsimd
            def _(pool):
                for k in range(CHUNKS):
                    pool.wait_ge(w_hi_done, k + 1)
                    nc.gpsimd.tensor_tensor(out=w_lo[k][:, :, :], in0=w_stage[:, k % 2, :].rearrange("p (c n) -> p c n", c=4),
                                            in1=w_hi[k][:, :, :].bitcast(F32), op=ALU.subtract).then_inc(w_lo_done, 1)

            @block.vector
            def _(dve):
                steps = [0]

                def link(ins):
                    steps[0] += 1
                    ins.then_inc(link_s, 1)
                    dve.wait_ge(link_s, steps[0])

                nc.vector.memset(ones[:, :], 1.0)
                nc.vector.memset(top[:, :], 0.0)
                low = 2 * (DIGITS - 1)
                for value in (1, 2, 3):
                    nc.vector.memset(digits[:, value - 1:value], value << low)
                nc.vector.memset(cands[:, 0:1], 1 << 30)
                link(nc.vector.memset(digit_one[:, :], float(1 << low)))
                dve.wait_ge(r_in, 32)

                def count_from(limit, j, seen):
                    nc.vector.tensor_scalar(out=seen[:, :], in0=sc[:, :], scalar1=limit, scalar2=0.0, op0=ALU.is_ge, op1=ALU.add,
                                            accum_out=count[:, j:j + 1]).then_inc(count_done, 1)

                count_from(0.0, 0, work)
                dve.wait_ge(total_done, 1)
                nc.vector.tensor_scalar(out=thr[:, :], in0=ps_tot[:, 0:1], scalar1=float(CAP), scalar2=-1.0, op0=ALU.is_lt,
                                        op1=ALU.mult).then_inc(thr_done, 1)
                dve.wait_ge(thr_done, 1)
                link(nc.vector.tensor_tensor(out=cands[:, 0:1], in0=thr[:, :], in1=cands[:, 0:1], op=ALU.bitwise_xor))
                count_from(cands[:, 0:1].bitcast(F32), 0, work)
                dve.wait_ge(total_done, 2)
                link(nc.vector.tensor_scalar(out=step[:, :], in0=ps_tot[:, 0:1], scalar1=float(CAP), scalar2=float(1 << 30), op0=ALU.is_ge,
                                             op1=ALU.mult))
                nc.vector.tensor_tensor(out=thr[:, :], in0=thr[:, :], in1=step[:, :], op=ALU.bitwise_xor).then_inc(thr_done, 1)
                with dve.Fori(1, DIGITS + 1) as i:
                    dve.wait_ge(thr_done, i + 1)
                    nc.vector.tensor_tensor(out=cands[:, :], in0=thr[:, :].broadcast_to([P, 3]), in1=digits[:, :], op=ALU.bitwise_xor).then_inc(cand_done, 1)
                    dve.wait_ge(cand_done, i)
                    for j, seen in enumerate((work, sel, eq)):
                        count_from(cands[:, j:j + 1].bitcast(F32), j, seen)
                    nc.vector.tensor_scalar(out=digits[:, :], in0=digits[:, :], scalar1=2, scalar2=None, op0=ALU.logical_shift_right).then_inc(bit_done, 1)
                    dve.wait_ge(total_done, i + 2)
                    nc.vector.tensor_scalar(out=reached[:, :], in0=ps_tot[:, 0:3], scalar1=float(CAP), scalar2=0.0, op0=ALU.is_ge,
                                            op1=ALU.add, accum_out=digit[:, :]).then_inc(digit_done, 1)
                    dve.wait_ge(digit_done, i)
                    nc.vector.tensor_scalar(out=step[:, :], in0=digit[:, :], scalar1=digit_one[:, :], scalar2=None, op0=ALU.mult).then_inc(step_done, 1)
                    dve.wait_ge(step_done, i)
                    nc.vector.tensor_scalar(out=digit_one[:, :], in0=digit_one[:, :], scalar1=0.25, scalar2=None, op0=ALU.mult).then_inc(bit_done, 1)
                    dve.wait_ge(bit_done, 2 * i)
                    nc.vector.tensor_tensor(out=thr[:, :], in0=thr[:, :], in1=step[:, :], op=ALU.bitwise_xor).then_inc(thr_done, 1)
                dve.wait_ge(thr_done, DIGITS + 2)
                limit = thr[:, :].bitcast(F32)
                nc.vector.tensor_scalar(out=sel[:, :], in0=sc[:, :], scalar1=limit, scalar2=0.0, op0=ALU.is_gt, op1=ALU.add,
                                        accum_out=stat[:, 0:1])
                link(nc.vector.tensor_scalar(out=eq[:, :], in0=sc[:, :], scalar1=limit, scalar2=0.0, op0=ALU.is_equal, op1=ALU.add,
                                             accum_out=stat[:, 1:2]))
                nc.vector.tensor_tensor_scan(out=rank[:, :], data0=ones[:, :], data1=eq[:, :], initial=0.0, op0=ALU.mult,
                                             op1=ALU.add).then_inc(asks, 1)
                dve.wait_ge(asks, 1)
                dve.wait_ge(answers, 1)
                link(nc.vector.tensor_scalar(out=stat[:, 3:4], in0=ps_a[:, 0:1], scalar1=-1.0, scalar2=float(CAP), op0=ALU.mult, op1=ALU.add))
                link(nc.vector.tensor_tensor(out=stat[:, 3:4], in0=stat[:, 3:4], in1=ps_a[:, 1:2], op=ALU.subtract))
                link(nc.vector.scalar_tensor_tensor(out=eq[:, :], in0=rank[:, :], scalar=stat[:, 3:4], in1=eq[:, :], op0=ALU.is_le, op1=ALU.mult))
                link(nc.vector.tensor_tensor(out=sel[:, :], in0=sel[:, :], in1=eq[:, :], op=ALU.add))
                link(nc.vector.tensor_tensor_scan(out=rank[:, :], data0=ones[:, :], data1=sel[:, :], initial=0.0, op0=ALU.mult, op1=ALU.add))
                nc.vector.tensor_copy(stat[:, 2:3], rank[:, S - 1:S])
                link(nc.vector.tensor_reduce(out=top[:, 0:1], in_=sc[:, :], axis=AX_X, op=ALU.max))
                nc.vector.tensor_scalar(out=work[:, :], in0=sel[:, :], scalar1=-512.0, scalar2=512.0, op0=ALU.mult, op1=ALU.add).then_inc(asks, 1)
                dve.wait_ge(asks, 2)
                dve.wait_ge(answers, 2)
                link(nc.vector.tensor_copy(stat[:, 6:7], ps_a[:, 0:1]))
                link(nc.vector.tensor_scalar(out=place_i[:, :], in0=rank[:, :], scalar1=stat[:, 6:7], scalar2=-1.0, op0=ALU.add, op1=ALU.add))
                link(nc.vector.tensor_reduce(out=top_row[0:1, 0, 0:E], in_=ps_a[0:1, P:2 * P].rearrange("o (b e) -> o e b", e=E), axis=AX_X, op=ALU.max))
                nc.vector.tensor_copy(top_row[0:1, 1, :].rearrange("o (b e) -> o b e", e=E),
                                      top_row[0:1, 0:1, 0:E].broadcast_to([1, B, E])).then_inc(asks, 1)
                dve.wait_ge(asks, 3)
                dve.wait_ge(answers, 3)
                nc.vector.tensor_scalar(out=stat[:, 4:5], in0=ps_a[:, 0:1], scalar1=-1.0, scalar2=None, op0=ALU.mult).then_inc(max_ready, 1)
                link(nc.vector.tensor_scalar(out=lo_i[:, :], in0=place_i[:, :], scalar1=P - 1, scalar2=None, op0=ALU.bitwise_and))
                link(nc.vector.tensor_scalar(out=hi_i[:, :], in0=place_i[:, :], scalar1=7, scalar2=None, op0=ALU.arith_shift_right))
                nc.vector.tensor_tensor(out=lo[:, :], in0=lo_i[:, :], in1=work[:, :], op=ALU.add).then_inc(lists_ready, 1)
                nc.vector.tensor_copy(hi[:, :], hi_i[:, :]).then_inc(lists_ready, 1)
                dve.wait_ge(ex_done, 1)
                link(nc.vector.tensor_tensor(out=ex[:, :], in0=ex[:, :], in1=sel[:, :], op=ALU.mult))
                nc.vector.tensor_reduce(out=stat[:, 5:6], in_=ex[:, :], axis=AX_X, op=ALU.add).then_inc(asks, 1)
                dve.wait_ge(answers, 4)
                link(nc.vector.reciprocal(stat[:, 7:8], ps_a[:, 0:1]))
                dve.wait_ge(lists_ready, 2)
                nc.vector.tensor_scalar(out=w[:, :], in0=ex[:, :], scalar1=stat[:, 7:8], scalar2=None, op0=ALU.mult).then_inc(lists_ready, 1)
                nc.vector.tensor_copy(numbers_b[:, :], numbers)

                def by_token(t):
                    return t.rearrange("p b c e -> p c b e")

                dve.wait_ge(listsT, 3)
                nc.vector.tensor_copy(by_token(loT[:, :, :, :]), ps_t[0][:, :, :].rearrange("p c (b e) -> p c b e", e=E))
                nc.vector.tensor_copy(by_token(hiT[:, :, :, :]), ps_t[1][:, :, :].rearrange("p c (b e) -> p c b e", e=E))
                rest = wrest[:, :, :].rearrange("p c (b e) -> p c b e", e=E)
                link(nc.vector.tensor_copy(rest, ps_t[2][:, :, :].rearrange("p c (b e) -> p c b e", e=E)))
                for i in range(3):
                    link(nc.vector.tensor_copy(by_token(wT[i][:, :, :, :]), rest))
                    if i < 2:
                        link(nc.vector.tensor_tensor(out=rest, in0=rest, in1=by_token(wT[i][:, :, :, :]), op=ALU.subtract))

        xg = sb("xg", [P, HTT, D])
        xT_hi = sb("exT_hi", [P, CT, HALF], F32R)
        xT_lo = sb("exT_lo", [P, CT, HALF], F32R)
        silu = sb("silu", [P, 2, HALF])
        g_f = sb("g_f", [P, 2, HALF])
        g_hi = sb("g_hi", [P, HT, HALF], F32R)
        g_lo = sb("g_lo", [P, HT, HALF], F32R)
        y = sb("y", [P, HTT, D])
        onehot = sb("onehot", [P, 2, GROUP, P], BF16)
        has_hi = sb("has_hi", [P, TILES, CAPT], BF16)
        payload = sb("payload", [P, TILES, PARTS, CAPT], BF16)
        lists = sb("lists", [P, PARTS, CAPT])
        idx_in = sb("idx_in", [P, CAPT], U32)
        idx_out = sb("idx_out", [P, CAPT], U32)
        w_next = sb("w_next", [P, CAPT])
        w_now = sb("w_now", [P, CAPT])
        w_sum = sb("w_sum", [P, CAPT])

        def psum(name, shape):
            return ctx.enter_context(nc.psum_tensor(name, shape, F32))

        ps_h = [[psum(f"ps_h{i}{j}", [P, HALF]) for j in range(2)] for i in range(2)]
        ps_y = [psum(f"ps_y{i}", [P, D]) for i in range(2)]
        ps_x = psum("ps_x", [P, CT, P])
        ps_lists = psum("ps_lists", [P, CT, P])
        ps_l = ps_lists[:, :, :].rearrange("p c q -> p (c q)")
        ps_first = (ps_x, ps_lists)

        has_done = sem("has_done")
        payload_done = sem("payload_done")
        onehot_done = sem("onehot_done")
        list_step = sem("list_step")
        lists_done = sem("lists_done")
        idx_done = sem("idx_done")
        wsum_done = sem("wsum_done")
        wnext_done = sem("wnext_done")
        now_done = sem("now_done")
        gathered = [sem(f"gathered{i}") for i in range(HTT)]
        xT_done = sem("xT_done")
        xThi_done, xTlo_done = sem("xThi_done"), sem("xTlo_done")
        h_done = sem("h_done")
        silu_done, g_f_done = sem("silu_done"), sem("g_f_done")
        g_hi_done, g_lo_done = sem("g_hi_done"), sem("g_lo_done")
        y_done = sem("y_done")
        y_ready = sem("y_ready")
        scattered = sem("scattered")
        pool_waited = sem("pool_waited")

        block = ctx.enter_context(nc.Block())

        def over_experts(eng, body):
            body(0, True, False)
            with eng.Fori(1, E - 1) as e:
                body(e, False, False)
            body(E - 1, False, True)

        def need(eng, s, value):
            if not (isinstance(value, int) and value <= 0):
                eng.wait_ge(s, value)

        @block.sync
        def _(sp):
            def body(e, first, last):
                if not last:
                    for k in range(CHUNKS):
                        load_w(sp, e + 1, k)

            over_experts(sp, body)

        @block.tensor
        def _(pe):
            def transpose_tile(e, i, bank=ps_x, banks=1):
                n = CAPT * e + i
                pe.wait_ge(gathered[i % HTT], 16 * (2 * e + i // HTT + 1))
                need(pe, xTlo_done, n + 1 - banks)
                for c in range(CT):
                    last = nc.tensor.matmul(bank[:, c, :], xg[:, i % HTT, c * P:(c + 1) * P], ident, is_transpose=True, start=True, stop=True)
                last.then_inc(xT_done, 1)

            def hidden(e, half, ht):
                n = 2 * HT * e + HT * half + ht
                if half == 0 and ht % 4 == 0:
                    pe.wait_ge(w_lo_done, CHUNKS * e + (2 if ht == 0 else 4))
                if ht == 0:
                    pe.wait_ge(xTlo_done, CAPT * e + HTT * (half + 1))
                need(pe, g_f_done, n - 1)
                f = slice((ht % 4) * P, (ht % 4 + 1) * P)
                for j in range(2):
                    k = 2 * (ht // 4) + j
                    for c in range(CT):
                        for i, (l, r) in enumerate(((w_hi[k], xT_hi), (w_hi[k], xT_lo), (w_lo[k], xT_hi))):
                            last = nc.tensor.matmul(ps_h[ht % 2][j][:, :], l[:, c, f], r[:, c, :], start=(c == 0 and i == 0),
                                                    stop=(c == CT - 1 and i == 2))
                last.then_inc(h_done, 1)

            def output(e, half, t):
                n = CAPT * e + HTT * half + t
                if half == 0 and t == 0:
                    pe.wait_ge(w_lo_done, CHUNKS * e + CHUNKS)
                need(pe, y_ready, n - 1)
                s = slice(t * P, (t + 1) * P)
                for ht in range(HT):
                    k, f = 4 + ht // 4, ht % 4
                    if t == 0:
                        pe.wait_ge(g_lo_done, 2 * HT * e + HT * half + ht + 1)
                    for i, (l, r) in enumerate(((g_hi, w_hi[k]), (g_hi, w_lo[k]), (g_lo, w_hi[k]))):
                        last = nc.tensor.matmul(ps_y[t % 2][:, :], l[:, ht, s], r[:, f, :], start=(ht == 0 and i == 0),
                                                stop=(ht == HT - 1 and i == 2))
                last.then_inc(y_done, 1)

            def list_part(e, q):
                pe.wait_ge(onehot_done, 4 * e + q + 1)
                if q == 0:
                    pe.wait_ge(payload_done, 5 * e + 5)
                    need(pe, lists_done, e)
                for t in range(GROUP):
                    n = q * GROUP + t
                    last = nc.tensor.matmul(ps_l[:, 0:PARTS * CAPT], onehot[:, q % 2, t, :],
                                            payload[:, n, :, :].rearrange("p k j -> p (k j)"), start=(n == 0), stop=(n == TILES - 1))
                last.then_inc(list_step, 1)

            for q in range(4):
                list_part(0, q)
            for i in range(HTT):
                transpose_tile(0, i, ps_first[i % 2], 2)

            def body(e, first, last):
                for half in range(2):
                    for ht in range(HT):
                        hidden(e, half, ht)
                        if half == 0 and not last and ht in (3, 4, 5, 6):
                            list_part(e + 1, ht - 3)
                    for t in range(HTT):
                        if half == 0:
                            transpose_tile(e, HTT + t)
                        elif not last:
                            transpose_tile(e + 1, t)
                        output(e, half, t)

            over_experts(pe, body)

        @block.scalar
        def _(act):
            def split_w(e, k):
                act.wait_ge(w_in[k % 2], 16 * (CHUNKS // 2 * e + k // 2 + 1))
                if k < 4:
                    act.wait_ge(h_done, 2 * HT * e - HT + (4 if k < 2 else 8))
                else:
                    need(act, y_done, CAPT * e)
                nc.scalar.activation(w_hi[k][:, :, :], w_stage[:, k % 2, :].rearrange("p (c n) -> p c n", c=4), ACT.Copy).then_inc(w_hi_done, 1)

            def tile_hi(e, i, bank=ps_x):
                s = slice((i % HTT) * P, (i % HTT + 1) * P)
                act.wait_ge(xT_done, CAPT * e + i + 1)
                nc.scalar.activation(xT_hi[:, :, s], bank[:, :, :], ACT.Copy).then_inc(xThi_done, 1)

            def gate(e, half, ht):
                n = 2 * HT * e + HT * half + ht
                act.wait_ge(h_done, n + 1)
                need(act, g_f_done, n - 1)
                nc.scalar.activation(silu[:, ht % 2, :], ps_h[ht % 2][0][:, :], ACT.Silu).then_inc(silu_done, 1)

            def hidden_hi(e, half, ht):
                n = 2 * HT * e + HT * half + ht
                act.wait_ge(g_f_done, n + 1)
                nc.scalar.activation(g_hi[:, ht, :], g_f[:, ht % 2, :], ACT.Copy).then_inc(g_hi_done, 1)

            for i in range(HTT):
                tile_hi(0, i, ps_first[i % 2])

            def body(e, first, last):
                for half in range(2):
                    for ht in range(HT):
                        gate(e, half, ht)
                        if ht == 0:
                            need(act, y_done, CAPT * e + HTT * half)
                        hidden_hi(e, half, ht)
                        if half == 0 and not first and ht in (1, 2):
                            split_w(e, 3 + ht)
                        if half == 1 and ht in (4, 5) and not last:
                            split_w(e + 1, ht - 4)
                    for t in range(HTT):
                        if half == 0:
                            tile_hi(e, HTT + t)
                        elif not last:
                            tile_hi(e + 1, t)
                            if t in (0, 1):
                                split_w(e + 1, 2 + t)

            over_experts(act, body)

        @block.vector
        def _(dve):
            def split_w(e, k):
                dve.wait_ge(w_hi_done, CHUNKS * e + k + 1)
                nc.vector.tensor_tensor(out=w_lo[k][:, :, :], in0=w_stage[:, k % 2, :].rearrange("p (c n) -> p c n", c=4),
                                        in1=w_hi[k][:, :, :].bitcast(F32), op=ALU.subtract).then_inc(w_lo_done, 1)

            def tile_lo(e, i, bank=ps_x):
                s = slice((i % HTT) * P, (i % HTT + 1) * P)
                dve.wait_ge(xThi_done, CAPT * e + i + 1)
                nc.vector.tensor_tensor(out=xT_lo[:, :, s], in0=bank[:, :, :], in1=xT_hi[:, :, s].bitcast(F32),
                                        op=ALU.subtract).then_inc(xTlo_done, 1)

            def gated(e, half, ht):
                n = 2 * HT * e + HT * half + ht
                dve.wait_ge(silu_done, n + 1)
                need(dve, g_hi_done, n - 1)
                nc.vector.tensor_tensor(out=g_f[:, ht % 2, :], in0=ps_h[ht % 2][1][:, :], in1=silu[:, ht % 2, :], op=ALU.mult).then_inc(g_f_done, 1)

            def hidden_lo(e, half, ht):
                n = 2 * HT * e + HT * half + ht
                dve.wait_ge(g_hi_done, n + 1)
                nc.vector.tensor_tensor(out=g_lo[:, ht, :], in0=g_f[:, ht % 2, :], in1=g_hi[:, ht, :].bitcast(F32),
                                        op=ALU.subtract).then_inc(g_lo_done, 1)

            def weigh(e, half, t):
                n = CAPT * e + HTT * half + t
                dve.wait_ge(y_done, n + 1)
                need(dve, scattered, 16 * (n - HTT + 1))
                if half == 0 and t == 0:
                    dve.wait_ge(now_done, 2 * e + 2)
                c = HTT * half + t
                nc.vector.tensor_scalar(out=y[:, t, :], in0=ps_y[t % 2][:, :], scalar1=w_now[:, c:c + 1], scalar2=None,
                                        op0=ALU.mult).then_inc(y_ready, 1)

            def make_payload(e):
                def over(t):
                    return t.rearrange("p b c e -> p (b c) e")[:, :, bass.ds(e, 1)].broadcast_to([P, TILES, CAPT])

                need(dve, list_step, 4 * e)
                nc.vector.tensor_tensor(out=has_hi[:, :, :], in0=over(hiT[:, :, :, :]),
                                        in1=numbers_b[:, 0:CAPT].rearrange("p (o j) -> p o j", o=1).broadcast_to([P, TILES, CAPT]),
                                        op=ALU.is_equal).then_inc(has_done, 1)
                dve.wait_ge(has_done, e + 1)
                ids = tile_ids.rearrange("p (n o) -> p n o", o=1).broadcast_to([P, TILES, CAPT])
                nc.vector.tensor_tensor(out=payload[:, :, 0, :], in0=has_hi[:, :, :], in1=ids, op=ALU.mult).then_inc(payload_done, 1)
                nc.vector.tensor_scalar(out=payload[:, :, 1, :], in0=has_hi[:, :, :], scalar1=row_id, scalar2=None, op0=ALU.mult).then_inc(payload_done, 1)
                for i in range(3):
                    nc.vector.tensor_tensor(out=payload[:, :, 2 + i, :], in0=has_hi[:, :, :], in1=over(wT[i][:, :, :, :]), op=ALU.mult).then_inc(payload_done, 1)

            def make_onehot(e, q):
                need(dve, list_step, 4 * e + q - 1)
                lo_q = loT[:, :, :, :].rearrange("p b c e -> p (b c) e")[:, q * GROUP:(q + 1) * GROUP, bass.ds(e, 1)].broadcast_to([P, GROUP, P])
                nc.vector.tensor_tensor(out=onehot[:, q % 2, :, :], in0=lo_q,
                                        in1=numbers_b[:, :].rearrange("p (o j) -> p o j", o=1).broadcast_to([P, GROUP, P]),
                                        op=ALU.is_equal).then_inc(onehot_done, 1)

            def read_lists(e):
                dve.wait_ge(list_step, 4 * e + 4)
                nc.vector.tensor_copy(lists[:, :, :], ps_l[:, 0:PARTS * CAPT].rearrange("p (k j) -> p k j", k=PARTS)).then_inc(lists_done, 1)
                dve.wait_ge(lists_done, e + 1)
                for i in range(HTT):
                    need(dve, gathered[i], 32 * e)
                need(dve, now_done, 2 * e)
                nc.vector.scalar_tensor_tensor(out=idx_in[:, :], in0=lists[:, 0, :], scalar=float(P), in1=lists[:, 1, :], op0=ALU.mult,
                                               op1=ALU.add).then_inc(idx_done, 1)
                nc.vector.tensor_tensor(out=w_sum[:, :], in0=lists[:, 2, :], in1=lists[:, 3, :], op=ALU.add).then_inc(wsum_done, 1)
                dve.wait_ge(wsum_done, e + 1)
                nc.vector.tensor_tensor(out=w_next[:, :], in0=w_sum[:, :], in1=lists[:, 4, :], op=ALU.add).then_inc(wnext_done, 1)

            def take_lists(e):
                dve.wait_ge(wnext_done, e + 1)
                need(dve, scattered, 16 * CAPT * e)
                nc.vector.tensor_copy(idx_out[:, :], idx_in[:, :]).then_inc(now_done, 1)
                nc.vector.tensor_copy(w_now[:, :], w_next[:, :]).then_inc(now_done, 1)

            make_payload(0)
            for q in range(4):
                make_onehot(0, q)
            read_lists(0)
            for i in range(HTT):
                tile_lo(0, i, ps_first[i % 2])

            def body(e, first, last):
                for half in range(2):
                    for ht in range(HT):
                        gated(e, half, ht)
                        hidden_lo(e, half, ht)
                        if half == 0:
                            if ht == 0:
                                take_lists(e)
                            if not first and ht in (1, 2):
                                split_w(e, 3 + ht)
                            if not last:
                                if ht == 0:
                                    make_payload(e + 1)
                                if ht in (1, 2, 4, 5):
                                    make_onehot(e + 1, ht - 1 if ht < 3 else ht - 2)
                                if ht == 7:
                                    read_lists(e + 1)
                        elif ht in (4, 5) and not last:
                            split_w(e + 1, ht - 4)
                    for t in range(HTT):
                        if half == 0:
                            tile_lo(e, HTT + t)
                        elif not last:
                            tile_lo(e + 1, t)
                            if t in (0, 1):
                                split_w(e + 1, 2 + t)
                        weigh(e, half, t)

            over_experts(dve, body)

        @block.gpsimd
        def _(pool):
            def gather(e, i):
                pool.wait_ge(idx_done, e + 1)
                need(pool, xT_done, CAPT * e + i - HTT + 1)
                pool.sem_inc(pool_waited, 1)
                pool.indirect_dma_start(out=xg[:, i % HTT, :], out_offset=None, in_=xn_dram,
                                        in_offset=bass.IndirectOffsetOnAxis(ap=idx_in[:, i:i + 1], axis=0)).then_inc(gathered[i % HTT], 16)

            def scatter(e, i):
                n = CAPT * e + i
                pool.wait_ge(now_done, 2 * e + 2)
                need(pool, scattered, 16 * n)
                pool.wait_ge(y_ready, n + 1)
                pool.sem_inc(pool_waited, 1)
                pool.indirect_dma_start(out=out, out_offset=bass.IndirectOffsetOnAxis(ap=idx_out[:, i:i + 1], axis=0), in_=y[:, i % HTT, :],
                                        in_offset=None, compute_op=ALU.add).then_inc(scattered, 16)

            for i in range(HTT):
                gather(0, i)

            def body(e, first, last):
                for i in range(HTT):
                    gather(e, HTT + i)
                for i in range(HTT):
                    scatter(e, i)
                if not last:
                    for i in range(HTT):
                        gather(e + 1, i)
                for i in range(HTT):
                    scatter(e, HTT + i)

            over_experts(pool, body)
            pool.wait_ge(scattered, 16 * CAPT * E)


def program(nc, x, ctx, mask, wq, wk, wv, wo, bq, bk, bv, bo, wg, weights, consts, out):
    B, S, D = x.shape
    E = wg.shape[2]
    xn = nc.dram_tensor("normed", [B * S, D], F32, kind="Internal").ap()
    router = nc.dram_tensor("router", [B * E, S], F32, kind="Internal").ap()
    q_parts, k_parts = (nc.dram_tensor(n, [D // P, P, 2, S], F32, kind="Internal").ap() for n in ("q_parts", "k_parts"))
    attention(nc, x, ctx, mask, {"q": wq, "k": wk, "v": wv, "o": wo}, bq, bk, bv, bo, wg, out,
              xn.rearrange("(b s) d -> b s d", b=B), router.rearrange("(b e) s -> b e s", b=B), q_parts, k_parts)
    experts(nc, xn, router, weights, consts, out.rearrange("b s d -> (b s) d"))


def kernel(x, ctx_1024, mask_Bx1x1xS2_if1, L0_xattn_wq, L0_xattn_bq, L0_xattn_wk, L0_xattn_bk, L0_xattn_wv, L0_xattn_bv,
           L0_xattn_wo, L0_xattn_bo, L0_ffn_Wg, L0_ffn_W1, L0_ffn_W2, L0_ffn_W3):
    from concourse import bacc
    from concourse.bass_utils import run_bass_kernel_spmd

    def host(a):
        return np.asarray(a)

    def by_feature(a):
        return host(a).reshape(-1, P).T

    def chunks_in(w):
        e, h, c = w.shape
        return w.reshape(e, h // 512, 512, c // P, P).transpose(0, 1, 4, 3, 2).reshape(e, h // 512, P, -1)

    def chunks_out(w):
        e, c, h = w.shape
        return w.reshape(e, c, h // 512, 4, P).transpose(0, 2, 4, 3, 1).reshape(e, h // 512, P, -1)

    x = host(x)
    B, S, D = x.shape
    w1, w3, w2 = chunks_in(host(L0_ffn_W1)), chunks_in(host(L0_ffn_W3)), chunks_out(host(L0_ffn_W2))
    wg = host(L0_ffn_Wg)
    E = wg.shape[0]
    arrays = {
        "x": x,
        "ctx": host(ctx_1024).transpose(0, 2, 1),
        "mask": host(mask_Bx1x1xS2_if1).reshape(B, S),
        "wq": host(L0_xattn_wq).T,
        "wk": host(L0_xattn_wk).T,
        "wv": host(L0_xattn_wv).T,
        "wo": host(L0_xattn_wo).T,
        "bq": by_feature(L0_xattn_bq),
        "bk": by_feature(L0_xattn_bk),
        "bv": by_feature(L0_xattn_bv),
        "bo": host(L0_xattn_bo),
        "wg": wg.T.reshape(D // P, P, E).transpose(1, 0, 2),
        "weights": np.stack([w1[:, 0], w3[:, 0], w1[:, 1], w3[:, 1], w2[:, 0], w2[:, 1]], axis=1),
        "consts": route_constants(B, E, S // P),
    }
    arrays = {f"in_{n}": np.ascontiguousarray(a) for n, a in arrays.items()}
    nc = bacc.Bacc("TRN2", target_bir_lowering=False, num_devices=1)
    args = [nc.dram_tensor(n, a.shape, mybir.dt.from_np(a.dtype), kind="ExternalInput").ap() for n, a in arrays.items()]
    out = nc.dram_tensor("out", x.shape, F32, kind="ExternalOutput").ap()
    program(nc, *args, out)
    return run_bass_kernel_spmd(nc, [arrays], core_ids=[0]).results[0]["out"]
```
